# Optimizing a Trainium2 kernel written in Bass

```python
import numpy as np
import jax
import jax.numpy as jnp

def _softmax(x, axis=-1):
    return jax.nn.softmax(x, axis=axis)

def _gelu(x):
    return jax.nn.gelu(x, approximate=True)

def _silu(x):
    return jax.nn.silu(x)

def _sigmoid(x):
    return jax.nn.sigmoid(x)

def _layernorm(x, axis=-1, eps=1e-05):
    m = jnp.mean(x, axis=axis, keepdims=True)
    v = jnp.var(x, axis=axis, keepdims=True)
    return (x - m) / jnp.sqrt(v + eps)

def _scatter_add(tgt, idx, src, axis=0):
    return tgt.at[idx].add(src)

def _segment_sum(src, seg, n):
    return jax.ops.segment_sum(src, seg, n)
kernel_name = 'mk_seq_preln_d1_jaxref_r8_58e057'

def setup_inputs(seed: int=0):
    np.random.seed(seed)
    _w = jnp.asarray

    def _L0_attn_setup():
        import jax, jax.numpy as jnp
        import numpy as np
        EMBED_DIM = 256
        NUM_HEADS = 16
        HEAD_DIM = EMBED_DIM // NUM_HEADS
        BATCH, SEQ = (4, 512)
        key = jax.random.key(seed)
        k1, k2, k3, k4 = jax.random.split(key, 4)
        scale = 1.0 / np.sqrt(EMBED_DIM)
        x = jax.random.normal(k1, (BATCH, SEQ, EMBED_DIM), dtype=jnp.float32)
        W_qkv = jax.random.normal(k2, (EMBED_DIM, 3 * EMBED_DIM), dtype=jnp.float32) * scale
        W_out = jax.random.normal(k3, (EMBED_DIM, EMBED_DIM), dtype=jnp.float32) * scale
        b_out = jax.random.normal(k4, (EMBED_DIM,), dtype=jnp.float32) * 0.01
        return {'x': x, 'W_qkv': W_qkv, 'W_out': W_out, 'b_out': b_out}
    _L0_attn_in = _L0_attn_setup()

    def _L0_ffn_setup():
        import jax, jax.numpy as jnp
        import numpy as np
        N_GROUPS = 4
        TOPK_GROUPS = 2
        TOPK = 4
        ROUTE_SCALE = 1.0

        def _gate(xt, gate_w):
            T = xt.shape[0]
            E = gate_w.shape[0]
            scores = jax.nn.sigmoid(xt @ gate_w.T)
            original_scores = scores
            sg = scores.reshape(T, N_GROUPS, E // N_GROUPS)
            group_scores = sg.max(axis=-1)
            _, gidx = jax.lax.top_k(group_scores, TOPK_GROUPS)
            gmask = jax.nn.one_hot(gidx, N_GROUPS, dtype=scores.dtype).sum(axis=1)
            masked = (sg * gmask[:, :, None]).reshape(T, E)
            _, idx = jax.lax.top_k(masked, TOPK)
            w = jnp.take_along_axis(original_scores, idx, axis=-1)
            w = w / w.sum(axis=-1, keepdims=True) * ROUTE_SCALE
            return (w, idx)
        key = jax.random.key(seed)
        ks = jax.random.split(key, 8)
        B, S, D = (1, 256, 256)
        E, I = (16, 176)
        SH = 2 * I
        s = 0.02
        return {'x': jax.random.normal(ks[0], (B, S, D), dtype=jnp.float32), 'gate_w': jax.random.normal(ks[1], (E, D), dtype=jnp.float32) * s, 'W1': jax.random.normal(ks[2], (E, I, D), dtype=jnp.float32) * s, 'W2': jax.random.normal(ks[3], (E, D, I), dtype=jnp.float32) * s, 'W3': jax.random.normal(ks[4], (E, I, D), dtype=jnp.float32) * s, 'Ws1': jax.random.normal(ks[5], (SH, D), dtype=jnp.float32) * s, 'Ws2': jax.random.normal(ks[6], (D, SH), dtype=jnp.float32) * s, 'Ws3': jax.random.normal(ks[7], (SH, D), dtype=jnp.float32) * s}
    _L0_ffn_in = _L0_ffn_setup()
    _d = {'L0_attn_x': _L0_attn_in['x'], 'L0_attn_W_qkv': _L0_attn_in['W_qkv'], 'L0_attn_W_out': _L0_attn_in['W_out'], 'L0_attn_b_out': _L0_attn_in['b_out'], 'L0_ffn_gate_w': _L0_ffn_in['gate_w'], 'L0_ffn_W1': _L0_ffn_in['W1'], 'L0_ffn_W2': _L0_ffn_in['W2'], 'L0_ffn_W3': _L0_ffn_in['W3'], 'L0_ffn_Ws1': _L0_ffn_in['Ws1'], 'L0_ffn_Ws2': _L0_ffn_in['Ws2'], 'L0_ffn_Ws3': _L0_ffn_in['Ws3']}
    _x0 = _d['L0_attn_x']
    _d['L0_attn_x'] = jax.random.normal(jax.random.fold_in(jax.random.key(seed), 1), (4, 1024, 256), dtype=_x0.dtype)
    del _x0
    return _d

def reference(L0_attn_x, L0_attn_W_qkv, L0_attn_W_out, L0_attn_b_out, L0_ffn_gate_w, L0_ffn_W1, L0_ffn_W2, L0_ffn_W3, L0_ffn_Ws1, L0_ffn_Ws2, L0_ffn_Ws3):

    def _L0_attn_ref(x, W_qkv, W_out, b_out):
        import jax, jax.numpy as jnp
        import numpy as np
        EMBED_DIM = 256
        NUM_HEADS = 16
        HEAD_DIM = EMBED_DIM // NUM_HEADS
        BATCH, SEQ = (4, 512)
        b, s, _ = x.shape
        qkv = (x @ W_qkv).reshape(b, s, 3, NUM_HEADS, HEAD_DIM)
        q, k, v = (qkv[:, :, 0], qkv[:, :, 1], qkv[:, :, 2])
        scores = jnp.einsum('bshd,bsHd->bshH', q, k) / jnp.sqrt(jnp.float32(HEAD_DIM))
        w = jax.nn.softmax(scores, axis=-1)
        attn = jnp.einsum('bshH,bsHd->bshd', w, v).reshape(b, s, EMBED_DIM)
        return attn @ W_out + b_out

    def _L0_ffn_ref(x, gate_w, W1, W2, W3, Ws1, Ws2, Ws3):
        import jax, jax.numpy as jnp
        import numpy as np
        N_GROUPS = 4
        TOPK_GROUPS = 2
        TOPK = 4
        ROUTE_SCALE = 1.0

        def _gate(xt, gate_w):
            T = xt.shape[0]
            E = gate_w.shape[0]
            scores = jax.nn.sigmoid(xt @ gate_w.T)
            original_scores = scores
            sg = scores.reshape(T, N_GROUPS, E // N_GROUPS)
            group_scores = sg.max(axis=-1)
            _, gidx = jax.lax.top_k(group_scores, TOPK_GROUPS)
            gmask = jax.nn.one_hot(gidx, N_GROUPS, dtype=scores.dtype).sum(axis=1)
            masked = (sg * gmask[:, :, None]).reshape(T, E)
            _, idx = jax.lax.top_k(masked, TOPK)
            w = jnp.take_along_axis(original_scores, idx, axis=-1)
            w = w / w.sum(axis=-1, keepdims=True) * ROUTE_SCALE
            return (w, idx)
        shape = x.shape
        D = shape[-1]
        xt = x.reshape(-1, D)
        E = W1.shape[0]
        weights, indices = _gate(xt, gate_w)
        combine = jnp.einsum('tk,tke->te', weights, jax.nn.one_hot(indices, E, dtype=weights.dtype))
        h1 = jnp.einsum('td,eid->tei', xt, W1)
        h3 = jnp.einsum('td,eid->tei', xt, W3)
        g = jax.nn.silu(h1) * h3 * combine[:, :, None]
        y = jnp.einsum('tei,edi->td', g, W2)
        z = jax.nn.silu(xt @ Ws1.T) * (xt @ Ws3.T) @ Ws2.T
        return (y + z).reshape(shape)
    x = L0_attn_x
    x = x + _L0_attn_ref(_layernorm(x, axis=-1), L0_attn_W_qkv, L0_attn_W_out, L0_attn_b_out)
    x = x + _L0_ffn_ref(_layernorm(x, axis=-1), L0_ffn_gate_w, L0_ffn_W1, L0_ffn_W2, L0_ffn_W3, L0_ffn_Ws1, L0_ffn_Ws2, L0_ffn_Ws3)
    return x

_drawn_inputs = setup_inputs


def setup_inputs(seed=0):
    import zlib

    import numpy as np

    out = dict(_drawn_inputs(seed))
    spreads = {}
    factors = {'L0_attn_b_out': 6.56,
     'L0_ffn_gate_w': 8.0,
     'L0_ffn_W1': 8.0,
     'L0_ffn_W2': 8.0,
     'L0_ffn_W3': 8.0,
     'L0_ffn_Ws1': 3.058,
     'L0_ffn_Ws2': 3.035,
     'L0_ffn_Ws3': 3.031}
    for name, (base, spread) in spreads.items():
        noise = np.random.default_rng([zlib.crc32(name.encode()), seed]).standard_normal(out[name].shape)
        drawn = base * np.exp(spread * noise) if base else spread * noise
        out[name] = jnp.asarray(drawn.astype(out[name].dtype))
    for name, factor in factors.items():
        out[name] = (out[name] * factor).astype(out[name].dtype)
    return out
```

```python
from contextlib import ExitStack

import concourse.bass as bass
from concourse import mybir

F32 = mybir.dt.float32
F32R = mybir.dt.float32r
ALU = mybir.AluOpType
ACT = mybir.ActivationFunctionType
AX = mybir.AxisListType

P = 128
T, D = 4096, 256
KD = D // P
HEADS, HD = 16, 16
E, I, SH = 16, 176, 352
ROWS = SH + E * I
TILES, TPB = T // P, 4
BLOCKS, BT = TILES // TPB, TPB * P
SHC = -(-SH // P)
EXC = E * I // P
NC = SHC + EXC
EPS = 1e-5
SLOTS_PER_PHASE = 6
GROUP = 4
NG = HEADS // GROUP
PROD = GROUP * HEADS * HD

CHUNK_AT = [c * P for c in range(SHC)] + [SH + c * P for c in range(EXC)]
CHUNK_ROWS = [min(P, SH - c * P) for c in range(SHC)] + [P] * EXC

AT_QKV = 0
AT_WO = AT_QKV + KD * 3 * D
AT_GATE = AT_WO + KD * D
AT_W1 = AT_GATE + KD * E
AT_W3 = AT_W1 + KD * ROWS
AT_W2 = AT_W3 + KD * ROWS
WCOLS = AT_W2 + NC * D
STAGE = 512
PIECES = -(-WCOLS // STAGE)
PIECES_ATT = -(-AT_W1 // STAGE)

SPANS = []
for _n in range(EXC):
    _r, _spans = _n * P, []
    while _r < (_n + 1) * P:
        _end = min((_n + 1) * P, (_r // I + 1) * I)
        _spans.append((_r // I, _r - _n * P, _end - _n * P))
        _r = _end
    SPANS.append(_spans)
CB_UPTO = [sum(len(SPANS[m]) for m in range(n % 2, n + 1, 2)) for n in range(EXC)]
CB_ALL = [sum(len(SPANS[m]) for m in range(r, EXC, 2)) for r in range(2)]

LAG = 2


class Block:

    def __init__(self, eng, i, parity):
        self.eng, self.i, self.parity, self.bases = eng, i, parity, {}

    def next(self):
        if isinstance(self.i, int):
            n = 2 * self.i + self.parity + 1
            return Block(self.eng, n // 2, n % 2)
        if self.parity == 0:
            after = Block(self.eng, self.i, 1)
            after.bases = self.bases
            return after
        return Shifted(self, 2)

    def count(self, per_block, offset):
        offset += per_block * self.parity
        if isinstance(self.i, int):
            return 2 * per_block * self.i + offset
        if per_block not in self.bases:
            self.bases[per_block] = self.eng.snap(self.i * (2 * per_block))
        return self.bases[per_block] + offset

    def is_first(self):
        return isinstance(self.i, int) and 2 * self.i + self.parity == 0

    def is_last(self):
        return isinstance(self.i, int) and 2 * self.i + self.parity == BLOCKS - 1


class Shifted(Block):

    def __init__(self, block, by):
        self.eng, self.i, self.parity, self.bases, self.by = block.eng, block.i, 0, block.bases, by

    def count(self, per_block, offset):
        return Block.count(self, per_block, offset + per_block * self.by)

    def next(self):
        raise AssertionError("two blocks ahead")


class Tile:

    def __init__(self, block, offset):
        self.block, self.offset = block, offset
        self.ring4, self.ring2 = offset % 4, offset % 2

    def done(self, back=0, per_tile=1, part=0):
        return self.block.count(4 * per_tile, per_tile * (self.offset + 1 - back) - part)

    def dma(self, rounds_back=0):
        return self.block.count(16, 16 * (self.offset // 4 + 1 - rounds_back))

    def exists(self):
        return not isinstance(self.block.i, int) or 0 <= self.number() < TILES

    def number(self):
        return 4 * (2 * self.block.i + self.block.parity) + self.offset


def wait(eng, sem, value):
    if not isinstance(value, int) or value > 0:
        eng.wait_ge(sem, value)


def slot_tiles(b, c):
    if c >= NC - 1:
        return None
    p = c // SLOTS_PER_PHASE
    return c % SLOTS_PER_PHASE, Tile(b, 5 + p), Tile(b, 4 + p), Tile(b, 6 + p)


def run(eng, prologue, slot, tail, rates=()):
    prologue(Block(eng, -1, 1))
    for c in range(LAG):
        slot(Block(eng, 0, 0), c)
    with eng.Fori(0, (BLOCKS - 2) // 2) as i:
        b = Block(eng, i, 0)
        for rate in rates:
            b.count(rate, 0)
        for _ in range(2):
            for c in range(LAG, NC):
                slot(b, c)
            after = b.next()
            for c in range(LAG):
                slot(after, c)
            b = after
    for n in range(BLOCKS - 2, BLOCKS):
        b = Block(eng, n // 2, n % 2)
        for c in range(LAG, NC):
            slot(b, c)
        if n < BLOCKS - 1:
            for c in range(LAG):
                slot(b.next(), c)
    tail(Block(eng, (BLOCKS - 1) // 2, (BLOCKS - 1) % 2))


def build(nc, x, weights, b_out, x1_dram, comb_dram, out):
    with ExitStack() as ctx:
        def sb(name, shape, dt=F32):
            return ctx.enter_context(nc.sbuf_tensor(name, shape, dt))

        def ps(name):
            return ctx.enter_context(nc.psum_tensor(name, [P, 512], F32))

        def sem(name):
            return ctx.enter_context(nc.semaphore(name))

        w_hi, w_lo = sb("w_hi", [P, WCOLS], F32R), sb("w_lo", [P, WCOLS], F32R)
        xt_hi = [sb(f"xt_hi{i}", [P, KD, BT], F32R) for i in range(2)]
        xt_lo = [sb(f"xt_lo{i}", [P, KD, BT], F32R) for i in range(2)]
        ident, bias = sb("ident", [P, P]), sb("bias", [P, D])
        g = [sb(f"g{i}", [P, BT]) for i in range(2)]
        g_hi = [sb(f"g_hi{i}", [P, BT], F32R) for i in range(2)]
        g_lo = [sb(f"g_lo{i}", [P, BT], F32R) for i in range(2)]
        cb = [sb(f"cb{i}", [P, BT]) for i in range(2)]
        xr = [sb(f"xr{i}", [P, D]) for i in range(TPB)]
        xs = [sb(f"xs{i}", [P, D]) for i in range(4)]
        xn = sb("xn", [P, D])
        nt_hi, nt_lo = sb("nt_hi", [P, KD * P], F32R), sb("nt_lo", [P, KD * P], F32R)
        qk = sb("qk", [P, 2 * D])
        vt = [sb(f"vt{i}", [P, D]) for i in range(2)]
        prod, score, att = sb("prod", [P, PROD]), sb("score", [P, D]), sb("att", [P, D])
        top, den, rden = sb("top", [P, HEADS]), sb("den", [P, HEADS]), sb("rden", [P, HEADS])
        stats = [sb(f"stats{i}", [P, 6]) for i in range(2)]
        mv = [sb(f"mv{i}", [P, 2]) for i in range(2)]
        var = [sb(f"var{i}", [P, 1]) for i in range(2)]
        rstd = [sb(f"rstd{i}", [P, 1]) for i in range(2)]
        neg_half = sb("neg_half", [P, 1])
        logit, sig = sb("logit", [P, TPB * E]), sb("sig", [P, TPB * E])
        gpick, epick = sb("gpick", [P, TPB, 10]), sb("epick", [P, TPB, 20])
        left = sb("left", [P, TPB, 20])
        best = sb("best", [P, TPB, 8])
        gsel, wsel = sb("gsel", [P, TPB * 4]), sb("wsel", [P, TPB * E])
        wden, hold = sb("wden", [P, TPB]), sb("hold", [P, 1])
        comb, comb_t = sb("comb", [P, E * TPB]), sb("comb_t", [E * TPB, P])

        h1 = [ps(f"h1_{i}") for i in range(2)]
        h3 = [ps(f"h3_{i}") for i in range(2)]
        y = [ps(f"y{i}") for i in range(2)]
        pa, pb = ps("pa"), ps("pb")

        consts = sem("consts")
        bias_in = sem("bias_in")
        piece_in = [sem(f"piece_in{i}") for i in range(4)]
        piece_hi, piece_lo = sem("piece_hi"), sem("piece_lo")
        x_in = [sem(f"x_in{i}") for i in range(4)]
        n_stats = [sem(f"n{i}_stats") for i in range(2)]
        n_mv = [sem(f"n{i}_mv") for i in range(2)]
        n_var = [sem(f"n{i}_var") for i in range(2)]
        n_rstd = [sem(f"n{i}_rstd") for i in range(2)]
        n_out = [sem(f"n{i}_out") for i in range(2)]
        n1t_ps, n1t_hi, n1t_lo = sem("n1t_ps"), sem("n1t_hi"), sem("n1t_lo")
        qk_ps, v_ps, qk_sb, v_sb = sem("qk_ps"), sem("v_ps"), sem("qk_sb"), sem("v_sb")
        prod_done, red_done = sem("prod_done"), sem("red_done")
        top_done, shifted, exp_done = sem("top_done"), sem("shifted"), sem("exp_done")
        den_done, rden_done, att_done = sem("den_done"), sem("rden_done"), sem("att_done")
        at_ps, at_hi, at_lo = sem("at_ps"), sem("at_hi"), sem("at_lo")
        proj_ps, xb_done, x1_done = sem("proj_ps"), sem("xb_done"), sem("x1_done")
        x1_out = [sem(f"x1_out{i}") for i in range(4)]
        n2t_ps, n2t_hi, n2t_lo = sem("n2t_ps"), sem("n2t_hi"), sem("n2t_lo")
        gate_ps, logit_done, gate_exp = sem("gate_ps"), sem("logit_done"), sem("gate_exp")
        route, comb_done = sem("route"), sem("comb_done")
        comb_ps, comb_sb, comb_out = sem("comb_ps"), sem("comb_sb"), sem("comb_out")
        h1_done, h3_done, silu_done = sem("h1_done"), sem("h3_done"), sem("silu_done")
        cb_in = [sem(f"cb_in{i}") for i in range(2)]
        weighted, g_done = sem("weighted"), sem("g_done")
        ghi_done, glo_done, down_done = sem("ghi_done"), sem("glo_done"), sem("down_done")
        xr_in = [sem(f"xr_in{i}") for i in range(TPB)]
        y_done = sem("y_done")
        y_out = [sem(f"y_out{i}") for i in range(TPB)]

        x_v = x.rearrange("(b j p) d -> b j p d", j=TPB, p=P)
        x1_v = x1_dram.rearrange("(b j p) d -> b j p d", j=TPB, p=P)
        out_v = out.rearrange("(b j p) d -> b j p d", j=TPB, p=P)
        stage = [g[0], g[1], cb[0], cb[1]]

        def piece_cols(k):
            return slice(k * STAGE, min((k + 1) * STAGE, WCOLS))

        def rows_of(view, tile):
            b = tile.block.count(1, tile.offset // 4)
            if isinstance(b, int):
                return view[b, tile.offset % 4]
            return view[bass.ds(b, 1), tile.offset % 4].rearrange("o p d -> (o p) d")

        def pieces_of_slot(n):
            first = PIECES_ATT + 2 * n
            return range(min(first, PIECES), min(first + 2, PIECES))

        def prologue_slots():
            return enumerate(range(-SLOTS_PER_PHASE, NC))

        block = ctx.enter_context(nc.Block())

        @block.sync
        def _(sp):
            def load_piece(k):
                wait(sp, piece_hi, k - 3)
                wait(sp, piece_lo, k - 3)
                cols = piece_cols(k)
                sp.dma_start(stage[k % 4][:, :cols.stop - cols.start], weights[:, cols]).then_inc(piece_in[k % 4], 16)

            def load_x(t):
                wait(sp, x1_out[t.ring4], t.dma(rounds_back=1))
                wait(sp, n_out[1], t.done(back=4))
                sp.dma_start(xs[t.ring4][:], rows_of(x_v, t)).then_inc(x_in[t.ring4], 16)

            def store_x1(t):
                wait(sp, x1_done, t.done())
                sp.dma_start(rows_of(x1_v, t), xs[t.ring4][:]).then_inc(x1_out[t.ring4], 16)

            def attention(b, c):
                if (st := slot_tiles(b, c)) is None:
                    return
                s, a, q, _ = st
                if s == 3 and q.exists():
                    store_x1(q)
                ahead = Tile(b, a.offset + 3)
                if s == 5 and q.exists() and ahead.exists():
                    load_x(ahead)

            def prologue(b):
                for n in range(4):
                    sp.dma_start(xs[n][:], x_v[0, n]).then_inc(x_in[n], 16)
                    load_piece(n)
                sp.dma_start(bias[:], b_out.partition_broadcast(P)).then_inc(bias_in, 16)
                for k in range(4, PIECES_ATT):
                    load_piece(k)
                for n, c in prologue_slots():
                    for k in pieces_of_slot(n):
                        load_piece(k)
                    attention(b, c)

            def load_weights_of_rows(b, n):
                for e, p0, p1 in SPANS[n]:
                    row = comb_dram[b.parity, e * TPB:(e + 1) * TPB, :].rearrange("j t -> (j t)")
                    sp.dma_start(cb[n % 2][p0:p1, :], row.partition_broadcast(p1 - p0)).then_inc(cb_in[n % 2], 16)

            def store_out(t):
                sp.wait_ge(y_done, t.done(back=-1))
                sp.dma_start(rows_of(out_v, t), xr[t.ring4][:]).then_inc(y_out[t.ring4], 16)

            def slot(b, c):
                if c == LAG - 1:
                    wait(sp, weighted, b.count(EXC, 0))
                    sp.wait_ge(comb_sb, b.count(1, 1))
                    sp.dma_start(comb_dram[b.parity], comb_t[:]).then_inc(comb_out, 16)
                    sp.wait_ge(comb_out, b.count(16, 16))
                    if b.is_first():
                        sp.wait_ge(piece_hi, PIECES)
                        sp.wait_ge(piece_lo, PIECES)
                    for n in range(2):
                        load_weights_of_rows(b, n)
                    if not b.is_first():
                        for j in range(TPB):
                            store_out(Tile(b, j - TPB))
                    for j in range(TPB):
                        wait(sp, y_out[j], b.count(16, 0))
                        sp.wait_ge(x1_out[j], b.count(16, 16))
                        sp.dma_start(xr[j][:], rows_of(x1_v, Tile(b, j))).then_inc(xr_in[j], 16)
                n = c + 1 - SHC
                if 2 <= n < EXC:
                    sp.wait_ge(weighted, b.count(EXC, n - 1))
                    load_weights_of_rows(b, n)
                attention(b, c)

            def tail(b):
                for j in range(TPB):
                    store_out(Tile(b, j))
                for j in range(TPB):
                    sp.wait_ge(y_out[j], 16 * BLOCKS)
                    sp.wait_ge(x1_out[j], 16 * BLOCKS)
                sp.wait_ge(comb_out, 16 * BLOCKS)

            run(sp, prologue, slot, tail, rates=(1, 4, 16, EXC))

        @block.scalar
        def _(act):
            def split_piece(k):
                cols = piece_cols(k)
                act.wait_ge(piece_in[k % 4], 16 * (k // 4 + 1))
                nc.scalar.activation(w_hi[:, cols], stage[k % 4][:, :cols.stop - cols.start],
                                     ACT.Copy).then_inc(piece_hi, 1)

            def n1t_hi_of(t):
                act.wait_ge(n1t_ps, t.done())
                wait(act, proj_ps, t.done(back=2))
                nc.scalar.activation(nt_hi[:], pa[:, :D], ACT.Copy).then_inc(n1t_hi, 1)

            def qkv_out(t):
                act.wait_ge(qk_ps, t.done())
                wait(act, shifted, t.done(back=1))
                nc.scalar.activation(qk[:], pb[:], ACT.Copy).then_inc(qk_sb, 1)
                act.wait_ge(v_ps, t.done())
                wait(act, att_done, t.done(back=2))
                nc.scalar.activation(vt[t.ring2][:].rearrange("p (d h) -> p h d", h=HEADS),
                                     pa[:, D:].rearrange("p (h d) -> p h d", h=HEADS),
                                     ACT.Copy).then_inc(v_sb, 1)

            def attention(b, c):
                if (st := slot_tiles(b, c)) is None:
                    return
                s, a, q, r = st
                if s == 0 and q.exists():
                    act.wait_ge(at_ps, q.done())
                    wait(act, v_ps, q.done(back=-1) if a.exists() else q.done())
                    nc.scalar.activation(nt_hi[:], pa[:, :D], ACT.Copy).then_inc(at_hi, 1)
                if s == 1 and r.exists():
                    n1t_hi_of(r)
                if s == 2 and a.exists():
                    act.wait_ge(shifted, a.done())
                    nc.scalar.activation(score[:], score[:], ACT.Exp, scale=float(HD) ** -0.5).then_inc(exp_done, 1)
                if s == 3 and r.exists():
                    qkv_out(r)
                if s == 4 and q.exists():
                    j = q.ring4
                    act.wait_ge(n2t_ps, q.done())
                    nc.scalar.activation(xt_hi[(b.parity + 1) % 2][:, :, j * P:(j + 1) * P],
                                         pa[:, :D].rearrange("p (k t) -> p k t", k=KD), ACT.Copy).then_inc(n2t_hi, 1)
                if s == 5 and q.exists():
                    j = q.ring4
                    act.wait_ge(gate_ps, q.done())
                    nc.scalar.activation(logit[:, j * E:(j + 1) * E], pb[:, :E], ACT.Copy).then_inc(logit_done, 1)

            def route_exp(b):
                act.wait_ge(logit_done, b.count(4, 8))
                wait(act, comb_done, b.count(1, 1))
                nc.scalar.activation(sig[:], logit[:], ACT.Exp, scale=-1.0).then_inc(gate_exp, 1)

            def prologue(b):
                for k in range(PIECES_ATT):
                    split_piece(k)
                first = Tile(b, 4)
                n1t_hi_of(first)
                qkv_out(first)
                for n, c in prologue_slots():
                    for k in pieces_of_slot(n):
                        split_piece(k)
                    attention(b, c)
                route_exp(b)

            def silu(b, c):
                n, r = CHUNK_ROWS[c], (b.parity + c) % 2
                act.wait_ge(h1_done, b.count(NC, c + 1))
                wait(act, glo_done, b.count(NC, c - 1))
                nc.scalar.activation(g[r][:n], h1[r][:n], ACT.Silu).then_inc(silu_done, 1)

            def ghi(b, c):
                n, r = CHUNK_ROWS[c], (b.parity + c) % 2
                act.wait_ge(g_done, b.count(NC, c + 1))
                nc.scalar.activation(g_hi[r][:n], g[r][:n], ACT.Copy).then_inc(ghi_done, 1)

            def ghi_before(b, c):
                if c > 0:
                    ghi(b, c - 1)
                elif not b.is_first():
                    n, r = CHUNK_ROWS[NC - 1], (b.parity + 1 + NC - 1) % 2
                    act.wait_ge(g_done, b.count(NC, 0))
                    nc.scalar.activation(g_hi[r][:n], g[r][:n], ACT.Copy).then_inc(ghi_done, 1)

            def slot(b, c):
                silu(b, c)
                ghi_before(b, c)
                attention(b, c)
                if c == 0:
                    act.wait_ge(comb_ps, b.count(1, 1))
                    wait(act, comb_out, b.count(16, 0))
                    nc.scalar.activation(comb_t[:], pb[:E * TPB, :P], ACT.Copy).then_inc(comb_sb, 1)
                if c == NC - 1 and not b.is_last():
                    route_exp(b)

            def tail(b):
                act.wait_ge(down_done, b.count(NC, NC - 2))
                ghi(b, NC - 1)

            run(act, prologue, slot, tail)

        @block.gpsimd
        def _(pool):
            def split_piece(k):
                cols = piece_cols(k)
                n = cols.stop - cols.start
                pool.wait_ge(piece_hi, k + 1)
                nc.gpsimd.tensor_tensor(w_lo[:, cols], stage[k % 4][:, :n], w_hi[:, cols].bitcast(F32),
                                        ALU.subtract).then_inc(piece_lo, 1)

            def rstd_of(norm, t):
                pool.wait_ge(n_var[norm], t.done())
                wait(pool, n_out[norm], t.done(back=1))
                nc.gpsimd.tensor_tensor(rstd[norm][:], var[norm][:], neg_half[:], ALU.pow).then_inc(n_rstd[norm], 1)

            def x_plus_bias(t):
                pool.wait_ge(n_out[0], t.done())
                nc.gpsimd.tensor_tensor(xs[t.ring4][:], xs[t.ring4][:], bias[:], ALU.add).then_inc(xb_done, 1)

            def attention(b, c):
                if (st := slot_tiles(b, c)) is None:
                    return
                s, _, q, r = st
                if s == 0 and r.exists():
                    rstd_of(0, r)
                if s == 2 and q.exists():
                    rstd_of(1, q)
                if s == 2 and r.exists():
                    x_plus_bias(r)

            def prologue(b):
                nc.gpsimd.memset(ident[:], 0.0).then_inc(consts, 1)
                nc.gpsimd.memset(neg_half[:], -0.5).then_inc(consts, 1)
                pool.wait_ge(consts, 2)
                pool.affine_select(out=ident[:], in_=ident[:], compare_op=ALU.not_equal, fill=1.0, base=0,
                                   pattern=[[-1, P]], channel_multiplier=1).then_inc(consts, 1)
                rstd_of(0, Tile(b, 4))
                pool.wait_ge(bias_in, 16)
                x_plus_bias(Tile(b, 4))
                for k in range(PIECES_ATT):
                    split_piece(k)
                for n, c in prologue_slots():
                    attention(b, c)
                    for k in pieces_of_slot(n):
                        split_piece(k)

            def glo(b, c, back=0):
                n, r = CHUNK_ROWS[c], (b.parity + back + c) % 2
                pool.wait_ge(ghi_done, b.count(NC, c + 1 - back * NC))
                nc.gpsimd.tensor_tensor(g_lo[r][:n], g[r][:n], g_hi[r][:n].bitcast(F32),
                                        ALU.subtract).then_inc(glo_done, 1)

            def slot(b, c):
                n, r = c - SHC, (b.parity + c) % 2
                if n >= 0:
                    pool.wait_ge(silu_done, b.count(NC, c + 1))
                    pool.wait_ge(cb_in[n % 2], b.count(16 * CB_ALL[n % 2], 16 * CB_UPTO[n]))
                    nc.gpsimd.tensor_tensor(g[r][:], g[r][:], cb[n % 2][:], ALU.mult).then_inc(weighted, 1)
                if c > 0:
                    glo(b, c - 1)
                elif not b.is_first():
                    glo(b, NC - 1, back=1)
                attention(b, c)

            def tail(b):
                glo(b, NC - 1)

            run(pool, prologue, slot, tail)

        @block.vector
        def _(dve):
            vec = nc.vector

            def carry_wait():
                vec.memset(hold[:], 0.0)

            def norm_stats(norm, t):
                vec.bn_stats(stats[norm][:], xs[t.ring4][:]).then_inc(n_stats[norm], 1)
                dve.wait_ge(n_stats[norm], t.done())
                carry_wait()
                vec.bn_aggr(mv[norm][:], stats[norm][:]).then_inc(n_mv[norm], 1)
                dve.wait_ge(n_mv[norm], t.done())
                vec.tensor_scalar(var[norm][:], mv[norm][:, 1:2], EPS, None, ALU.add).then_inc(n_var[norm], 1)

            def norm_out(norm, t):
                dve.wait_ge(n_rstd[norm], t.done())
                vec.tensor_scalar(xn[:], xs[t.ring4][:], mv[norm][:, 0:1], rstd[norm][:, 0:1],
                                  ALU.subtract, ALU.mult).then_inc(n_out[norm], 1)

            def n1t_lo_of(t):
                dve.wait_ge(n1t_hi, t.done())
                vec.tensor_tensor(nt_lo[:], pa[:, :D], nt_hi[:].bitcast(F32), ALU.subtract).then_inc(n1t_lo, 1)

            def product(t, n):
                i = n % NG
                heads = slice(i * GROUP * HD, (i + 1) * GROUP * HD)
                if n == 0:
                    dve.wait_ge(qk_sb, t.done())
                if n == NG:
                    dve.wait_ge(exp_done, t.done())
                    dve.wait_ge(v_sb, t.done())
                wait(dve, red_done, t.done(per_tile=2 * NG, part=2 * NG - n))
                left = (qk[:, heads] if n < NG else score[:, heads]).rearrange("p (h d) -> p h d", h=GROUP)
                right = (qk[:, D:] if n < NG else vt[t.ring2][:]).rearrange("p (h d) -> p h d", h=HEADS)
                shape = [P, GROUP, HEADS, HD]
                vec.tensor_tensor(prod[:].rearrange("p (g h d) -> p g h d", g=GROUP, h=HEADS),
                                  left[:, :, None, :].broadcast_to(shape), right[:, None, :, :].broadcast_to(shape),
                                  ALU.mult).then_inc(prod_done, 1)

            def reduced(t, n):
                i = n % NG
                to = (score if n < NG else att)[:, i * GROUP * HD:(i + 1) * GROUP * HD]
                dve.wait_ge(prod_done, t.done(per_tile=2 * NG, part=2 * NG - 1 - n))
                if n == NG:
                    wait(dve, at_ps, t.done(back=1))
                vec.tensor_reduce(to, prod[:].rearrange("p (x d) -> p x d", d=HD), AX.X, ALU.add).then_inc(red_done, 1)

            def shift(t):
                s3 = score[:].rearrange("p (h g) -> p h g", h=HEADS)
                dve.wait_ge(red_done, t.done(per_tile=2 * NG, part=NG))
                vec.tensor_reduce(top[:], s3, AX.X, ALU.max).then_inc(top_done, 1)
                dve.wait_ge(top_done, t.done())
                vec.tensor_tensor(s3, s3, top[:, :, None].broadcast_to([P, HEADS, HEADS]),
                                  ALU.subtract).then_inc(shifted, 1)

            def denominator(t):
                dve.wait_ge(exp_done, t.done())
                vec.tensor_reduce(den[:], score[:].rearrange("p (h g) -> p h g", h=HEADS), AX.X,
                                  ALU.add).then_inc(den_done, 1)
                dve.wait_ge(den_done, t.done())
                vec.reciprocal(rden[:], den[:]).then_inc(rden_done, 1)

            def normalise(t):
                a3 = att[:].rearrange("p (h d) -> p h d", h=HEADS)
                dve.wait_ge(red_done, t.done(per_tile=2 * NG))
                dve.wait_ge(rden_done, t.done())
                vec.tensor_tensor(a3, a3, rden[:, :, None].broadcast_to([P, HEADS, HD]),
                                  ALU.mult).then_inc(att_done, 1)

            def attention(b, c):
                if (st := slot_tiles(b, c)) is None:
                    return
                s, a, q, r = st
                if s == 0:
                    if a.exists():
                        product(a, 0)
                        reduced(a, 0)
                        product(a, 1)
                    if r.exists():
                        dve.wait_ge(x_in[r.ring4], r.dma())
                        norm_stats(0, r)
                if s == 1:
                    if q.exists():
                        dve.wait_ge(at_hi, q.done())
                        vec.tensor_tensor(nt_lo[:], pa[:, :D], nt_hi[:].bitcast(F32), ALU.subtract).then_inc(at_lo, 1)
                    if a.exists():
                        reduced(a, 1)
                    if r.exists():
                        norm_out(0, r)
                    if a.exists():
                        product(a, 2)
                        reduced(a, 2)
                if s == 2:
                    if a.exists():
                        product(a, 3)
                        reduced(a, 3)
                        shift(a)
                    if q.exists():
                        dve.wait_ge(proj_ps, q.done())
                        dve.wait_ge(xb_done, q.done())
                        vec.tensor_tensor(xs[q.ring4][:], pb[:, :D], xs[q.ring4][:], ALU.add).then_inc(x1_done, 1)
                        dve.wait_ge(x1_done, q.done())
                        norm_stats(1, q)
                    if r.exists():
                        wait(dve, proj_ps, q.done() if q.exists() else 0)
                        n1t_lo_of(r)
                if s == 3:
                    if q.exists():
                        norm_out(1, q)
                    if a.exists():
                        denominator(a)
                        product(a, 4)
                        reduced(a, 4)
                        product(a, 5)
                if s == 4 and a.exists():
                    reduced(a, 5)
                    product(a, 6)
                    reduced(a, 6)
                if s == 5:
                    if q.exists():
                        j = q.ring4
                        dve.wait_ge(n2t_hi, q.done())
                        part = (slice(None), slice(None), slice(j * P, (j + 1) * P))
                        vec.tensor_tensor(xt_lo[(b.parity + 1) % 2][part], pa[:, :D].rearrange("p (k t) -> p k t", k=KD),
                                          xt_hi[(b.parity + 1) % 2][part].bitcast(F32), ALU.subtract).then_inc(n2t_lo, 1)
                    if a.exists():
                        product(a, 7)
                        reduced(a, 7)
                        normalise(a)

            ROUTE = 14

            def routing(b):
                step = [0]

                def then(ins):
                    step[0] += 1
                    ins.then_inc(route, 1)

                def after_last():
                    dve.wait_ge(route, b.count(ROUTE, ROUTE + step[0]))

                dve.wait_ge(gate_exp, b.count(1, 2))
                then(vec.tensor_scalar(sig[:], sig[:], 1.0, None, ALU.add))
                after_last()
                then(vec.reciprocal(sig[:], sig[:]))
                after_last()
                then(vec.tensor_reduce(gpick[:, :, 0:4], sig[:].rearrange("p (j g e) -> p j g e", j=TPB, g=4), AX.X, ALU.max))
                after_last()
                carry_wait()
                for j in range(TPB):
                    last = vec.max(best[:, j], gpick[:, j])
                then(last)
                after_last()
                then(vec.memset(best[:, :, 2:], -1.0))
                after_last()
                carry_wait()
                for j in range(TPB):
                    last = vec.match_replace(left[:, j, 0:10], best[:, j], gpick[:, j], -9.0)
                then(last)
                after_last()
                then(vec.tensor_scalar(gsel[:].rearrange("p (j g) -> p j g", j=TPB), left[:, :, 0:4], -2.0, None, ALU.is_lt))
                after_last()
                then(vec.tensor_tensor(epick[:, :, 0:E].rearrange("p j (g e) -> p j g e", g=4),
                                       sig[:].rearrange("p (j g e) -> p j g e", j=TPB, g=4),
                                       gsel[:].rearrange("p (j g) -> p j g", j=TPB)[:, :, :, None].broadcast_to([P, TPB, 4, 4]),
                                       ALU.mult))
                after_last()
                carry_wait()
                for j in range(TPB):
                    last = vec.max(best[:, j], epick[:, j])
                then(last)
                after_last()
                then(vec.memset(best[:, :, 4:], -1.0))
                after_last()
                carry_wait()
                for j in range(TPB):
                    last = vec.match_replace(left[:, j], best[:, j], epick[:, j], -9.0)
                then(last)
                after_last()
                w3 = wsel[:].rearrange("p (j e) -> p j e", j=TPB)
                then(vec.scalar_tensor_tensor(w3, left[:, :, 0:E], -2.0, sig[:].rearrange("p (j e) -> p j e", j=TPB),
                                              ALU.is_lt, ALU.mult))
                after_last()
                then(vec.tensor_reduce(wden[:], w3, AX.X, ALU.add))
                after_last()
                then(vec.reciprocal(wden[:], wden[:]))
                after_last()
                wait(dve, comb_ps, b.count(1, 1))
                vec.tensor_tensor(comb[:].rearrange("p (e j) -> p j e", j=TPB), w3,
                                  wden[:, :, None].broadcast_to([P, TPB, E]), ALU.mult).then_inc(comb_done, 1)
                assert step[0] == ROUTE

            def prologue(b):
                vec.memset(gpick[:, :, 4:], -1.0)
                vec.memset(epick[:, :, E:], -1.0).then_inc(y_done, 1)
                first = Tile(b, 4)
                dve.wait_ge(x_in[0], 16)
                dve.wait_ge(consts, 3)
                norm_stats(0, first)
                norm_out(0, first)
                n1t_lo_of(first)
                for n, c in prologue_slots():
                    attention(b, c)
                routing(b)

            def finish(b, back=0):
                dve.wait_ge(down_done, b.count(NC, NC - NC * back))
                for j in range(TPB):
                    dve.wait_ge(xr_in[j], b.count(16, 16 - 16 * back))
                    vec.tensor_tensor(xr[j][:], y[j // 2][:, j % 2 * D:(j % 2 + 1) * D], xr[j][:],
                                      ALU.add).then_inc(y_done, 1)

            def slot(b, c):
                n, r = CHUNK_ROWS[c], (b.parity + c) % 2
                attention(b, c)
                if c == NC - 1 and not b.is_last():
                    routing(b)
                dve.wait_ge(h3_done, b.count(NC, c + 1))
                if c < SHC:
                    dve.wait_ge(silu_done, b.count(NC, c + 1))
                else:
                    dve.wait_ge(weighted, b.count(EXC, c + 1 - SHC))
                vec.tensor_tensor(g[r][:n], g[r][:n], h3[r][:n], ALU.mult).then_inc(g_done, 1)
                if c == LAG - 1 and not b.is_first():
                    finish(b, back=1)

            run(dve, prologue, slot, finish)

        @block.tensor
        def _(pe):
            mm = nc.tensor.matmul

            def product(to, left_hi, left_lo, right_hi, right_lo, **kw):
                terms = [(lh, rh) for lh, rh in ((left_hi, right_hi), (left_hi, right_lo), (left_lo, right_hi))]
                for n, (lh, rh) in enumerate(terms):
                    for k in range(KD):
                        last = mm(to, lh(k), rh(k), start=(n == 0 and k == 0), stop=(n == 2 and k == KD - 1), **kw)
                return last

            def cols(w, at, k, width, first, count):
                return w[:, at + k * width + first:at + k * width + first + count]

            def transposes(src):
                for k in range(KD):
                    last = nc.tensor.transpose(pa[:, k * P:(k + 1) * P], src[:, k * P:(k + 1) * P], ident[:])
                return last

            def n1_transposed(t):
                pe.wait_ge(n_out[0], t.done())
                wait(pe, v_sb, t.done(back=1))
                transposes(xn).then_inc(n1t_ps, 1)

            def qkv(t):
                pe.wait_ge(n1t_lo, t.done())
                hi, lo = (lambda k: nt_hi[:, k * P:(k + 1) * P]), (lambda k: nt_lo[:, k * P:(k + 1) * P])
                for to, first, count, done in ((pb[:], 0, 2 * D, qk_ps), (pa[:, D:], 2 * D, D, v_ps)):
                    product(to, hi, lo, lambda k: cols(w_hi, AT_QKV, k, 3 * D, first, count),
                            lambda k: cols(w_lo, AT_QKV, k, 3 * D, first, count)).then_inc(done, 1)

            def attention(b, c):
                if (st := slot_tiles(b, c)) is None:
                    return
                s, a, q, r = st
                if s == 0 and q.exists():
                    pe.wait_ge(att_done, q.done())
                    if Tile(b, q.offset - 1).exists():
                        wait(pe, n2t_lo, q.done(back=1))
                    else:
                        pe.wait_ge(v_sb, q.done(back=-1))
                    transposes(att).then_inc(at_ps, 1)
                if s == 1:
                    if q.exists():
                        pe.wait_ge(at_lo, q.done())
                        wait(pe, logit_done, q.done(back=1))
                        if a.exists():
                            pe.wait_ge(qk_sb, a.done())
                        if c == 1:
                            wait(pe, comb_sb, b.count(1, 1))
                        product(pb[:, :D], lambda k: nt_hi[:, k * P:(k + 1) * P], lambda k: nt_lo[:, k * P:(k + 1) * P],
                                lambda k: cols(w_hi, AT_WO, k, D, 0, D),
                                lambda k: cols(w_lo, AT_WO, k, D, 0, D)).then_inc(proj_ps, 1)
                    if r.exists():
                        n1_transposed(r)
                if s == 2 and r.exists():
                    if q.exists():
                        pe.wait_ge(x1_done, q.done())
                    else:
                        wait(pe, qk_sb, r.done(back=1))
                    qkv(r)
                if s == 4 and q.exists():
                    pe.wait_ge(n_out[1], q.done())
                    if r.exists():
                        pe.wait_ge(v_sb, r.done())
                    transposes(xn).then_inc(n2t_ps, 1)
                if s == 5 and q.exists():
                    j, par = q.ring4, (b.parity + 1) % 2
                    pe.wait_ge(n2t_lo, q.done())
                    if r.exists():
                        pe.wait_ge(qk_sb, r.done())
                    product(pb[:, :E], lambda k: xt_hi[par][:, k, j * P:(j + 1) * P],
                            lambda k: xt_lo[par][:, k, j * P:(j + 1) * P],
                            lambda k: cols(w_hi, AT_GATE, k, E, 0, E),
                            lambda k: cols(w_lo, AT_GATE, k, E, 0, E)).then_inc(gate_ps, 1)

            def prologue(b):
                first = Tile(b, 4)
                pe.wait_ge(consts, 3)
                n1_transposed(first)
                pe.wait_ge(piece_lo, PIECES_ATT)
                qkv(first)
                for n, c in prologue_slots():
                    attention(b, c)
                pe.wait_ge(piece_lo, PIECES)

            def rows(b, c):
                n, at, r, par = CHUNK_ROWS[c], CHUNK_AT[c], (b.parity + c) % 2, b.parity
                if c == 0:
                    pe.wait_ge(n2t_lo, b.count(4, 4))
                for to, w_at, freed, done in ((h1[r], AT_W1, silu_done, h1_done), (h3[r], AT_W3, g_done, h3_done)):
                    wait(pe, freed, b.count(NC, c - 1))
                    product(to[:n], lambda k: cols(w_hi, w_at, k, ROWS, at, n), lambda k: cols(w_lo, w_at, k, ROWS, at, n),
                            lambda k: xt_hi[par][:, k, :], lambda k: xt_lo[par][:, k, :]).then_inc(done, 1)

            def down(b, c, back=0):
                n, r = CHUNK_ROWS[c], (b.parity + back + c) % 2
                pe.wait_ge(glo_done, b.count(NC, c + 1 - back * NC))
                if c == 0:
                    pe.wait_ge(y_done, b.count(4, 1))
                w = slice(AT_W2 + c * D, AT_W2 + (c + 1) * D)
                for j in range(TPB):
                    tok = slice(j * P, (j + 1) * P)
                    for m, (gp, wp) in enumerate(((g_hi, w_hi), (g_hi, w_lo), (g_lo, w_hi))):
                        last = mm(y[j // 2][:, j % 2 * D:(j % 2 + 1) * D], gp[r][:n, tok], wp[:n, w],
                                  start=(c == 0 and j % 2 == 0 and m == 0),
                                  stop=(c == NC - 1 and j % 2 == 1 and m == 2), skip_group_check=True)
                last.then_inc(down_done, 1)

            def slot(b, c):
                rows(b, c)
                if c >= LAG:
                    down(b, c - LAG)
                elif not b.is_first():
                    down(b, NC + c - LAG, back=1)
                attention(b, c)
                if c == 0:
                    pe.wait_ge(comb_done, b.count(1, 1))
                    pe.wait_ge(logit_done, b.count(4, 4))
                    mm(pb[:E * TPB, :P], comb[:], ident[:], start=True, stop=True).then_inc(comb_ps, 1)

            def tail(b):
                for c in range(NC - LAG, NC):
                    down(b, c)

            run(pe, prologue, slot, tail)


def kernel(L0_attn_x, L0_attn_W_qkv, L0_attn_W_out, L0_attn_b_out, L0_ffn_gate_w, L0_ffn_W1, L0_ffn_W2,
           L0_ffn_W3, L0_ffn_Ws1, L0_ffn_Ws2, L0_ffn_Ws3):
    import numpy as np
    import concourse.bacc as bacc
    from concourse.bass_utils import run_bass_kernel_spmd

    def by_contraction(w):
        w = np.asarray(w)
        return w.reshape(KD, P, w.shape[1]).transpose(1, 0, 2).reshape(P, -1)

    def up(shared, routed):
        return by_contraction(np.concatenate([np.asarray(shared), np.asarray(routed).reshape(E * I, D)]).T)

    ws2 = np.asarray(L0_ffn_Ws2).T
    w2 = np.asarray(L0_ffn_W2).transpose(0, 2, 1).reshape(E * I, D)
    pad = np.zeros((SHC * P - SH, D), ws2.dtype)
    down = np.concatenate([ws2, pad, w2]).reshape(NC, P, D).transpose(1, 0, 2).reshape(P, NC * D)
    packed = np.concatenate([by_contraction(L0_attn_W_qkv), by_contraction(L0_attn_W_out),
                             by_contraction(np.asarray(L0_ffn_gate_w).T), up(L0_ffn_Ws1, L0_ffn_W1),
                             up(L0_ffn_Ws3, L0_ffn_W3), down], axis=1)
    assert packed.shape == (P, WCOLS)
    arrays = {
        "x": np.ascontiguousarray(np.asarray(L0_attn_x).reshape(T, D)),
        "weights": np.ascontiguousarray(packed),
        "b_out": np.ascontiguousarray(np.asarray(L0_attn_b_out)),
    }
    nc = bacc.Bacc("TRN2", target_bir_lowering=False, num_devices=1, dynamic_dma_scratch_size=1024)
    ins = [nc.dram_tensor(n, a.shape, mybir.dt.from_np(a.dtype), kind="ExternalInput").ap() for n, a in arrays.items()]
    x1 = nc.dram_tensor("x1", (T, D), F32, kind="Internal").ap()
    comb = nc.dram_tensor("comb_by_expert", (2, E * TPB, P), F32, kind="Internal").ap()
    out = nc.dram_tensor("out", (T, D), F32, kind="ExternalOutput").ap()
    build(nc, *ins, x1, comb, out)
    r = run_bass_kernel_spmd(nc, [arrays], core_ids=[0])
    return r.results[0]["out"].reshape(np.asarray(L0_attn_x).shape)
```

```python
from contextlib import ExitStack

import concourse.bass as bass
from concourse import mybir

F32 = mybir.dt.float32
F32R = mybir.dt.float32r
ALU = mybir.AluOpType
ACT = mybir.ActivationFunctionType
AX = mybir.AxisListType

P = 128
T, D = 4096, 256
KD = D // P
HEADS, HD = 16, 16
E, I, SH = 16, 176, 352
TILES, TPB = T // P, 2
BLOCKS, BT = TILES // TPB, TPB * P
TPP = 2 * TPB
SHC = -(-SH // P)
EXC = E * I // P
NC = SHC + EXC
RING = 5
EPS = 1e-5
PHASE = 12
GROUP = 4
NG = HEADS // GROUP
PROD = GROUP * HEADS * HD

CHUNK_ROWS = [min(P, SH - c * P) for c in range(SHC)] + [P] * EXC

AT_QKV = 0
AT_WO = AT_QKV + KD * 3 * D
AT_GATE = AT_WO + KD * D
AT_CHUNK = [AT_GATE + KD * E]
for _rows in CHUNK_ROWS:
    AT_CHUNK.append(AT_CHUNK[-1] + 2 * KD * _rows + D)
WCOLS = AT_CHUNK[-1]
STAGE = 512


def pieces_until(col):
    return -(-col // STAGE)


PIECES = pieces_until(WCOLS)
PIECES_ATT = pieces_until(AT_CHUNK[0])

SPANS = {}
for _n in range(EXC):
    _r, _spans = _n * P, []
    while _r < (_n + 1) * P:
        _end = min((_n + 1) * P, (_r // I + 1) * I)
        _spans.append((_r // I, _r - _n * P, _end - _n * P))
        _r = _end
    SPANS[SHC + _n] = _spans
CB_UPTO = {c: sum(len(SPANS[m]) for m in SPANS if m % RING == c % RING and m <= c) for c in SPANS}
CB_ALL = [sum(len(SPANS[m]) for m in SPANS if m % RING == r) for r in range(RING)]

LAG = 3
LAST = 4
PEEL = RING


class Block:

    def __init__(self, eng, i, parity, bases=None, pairs_on=0):
        self.eng, self.i, self.parity, self.pairs_on = eng, i, parity, pairs_on
        self.bases = {} if bases is None else bases

    def next(self):
        if isinstance(self.i, int):
            n = 2 * self.i + self.parity + 1
            return Block(self.eng, n // 2, n % 2)
        return Block(self.eng, self.i, 1 - self.parity, self.bases, self.pairs_on + self.parity)

    def of_pair(self, per_pair, offset):
        if isinstance(self.i, int):
            return per_pair * self.i + offset
        if per_pair not in self.bases:
            self.bases[per_pair] = self.eng.snap(self.i * per_pair)
        return self.bases[per_pair] + (offset + per_pair * self.pairs_on)

    def count(self, per_block, offset):
        return self.of_pair(2 * per_block, offset + per_block * self.parity)

    def number(self):
        return 2 * self.i + self.parity if isinstance(self.i, int) else None


class Tile:

    def __init__(self, block, offset):
        self.block, self.offset = block, offset
        self.in_pair = TPB * block.parity + offset
        self.ring4, self.ring2 = self.in_pair % TPP, offset % 2

    def done(self, back=0, per_tile=1, part=0):
        return self.block.count(TPB * per_tile, per_tile * (self.offset + 1 - back) - part)

    def dma(self):
        return self.block.of_pair(16, 16 * (self.in_pair // TPP + 1))

    def number(self):
        n = self.block.number()
        return None if n is None else TPB * n + self.offset

    def exists(self):
        return self.number() is None or 0 <= self.number() < TILES


def wait(eng, sem, value):
    if not isinstance(value, int) or value > 0:
        eng.wait_ge(sem, value)


def slot_tiles(b, c):
    if c >= 2 * PHASE:
        return None
    p = c // PHASE
    return c % PHASE, Tile(b, 2 + p), Tile(b, 3 + p), Tile(b, 4 + p)


def behind(b, c, lag):
    return b.number() != 0 or c >= lag, CHUNK_ROWS[(c - lag) % NC], (c - lag) % RING


def run(eng, prologue, slot, tail, rates=()):
    prologue(Block(eng, -1, 1))
    for c in range(PEEL):
        slot(Block(eng, 0, 0), c)
    with eng.Fori(0, (BLOCKS - LAST) // 2) as i:
        b = Block(eng, i, 0)
        for rate in rates:
            b.of_pair(rate, 0)
        for _ in range(2):
            for c in range(PEEL, NC):
                slot(b, c)
            b = b.next()
            for c in range(PEEL):
                slot(b, c)
    for n in range(BLOCKS - LAST, BLOCKS):
        b = Block(eng, n // 2, n % 2)
        for c in range(PEEL, NC):
            slot(b, c)
        if n < BLOCKS - 1:
            for c in range(PEEL):
                slot(b.next(), c)
    tail(Block(eng, BLOCKS // 2, 0))


def build(nc, x, weights, b_out, comb_dram, out):
    with ExitStack() as ctx:
        def sb(name, shape, dt=F32):
            return ctx.enter_context(nc.sbuf_tensor(name, shape, dt))

        def ps(name):
            return ctx.enter_context(nc.psum_tensor(name, [P, 512], F32))

        def sem(name):
            return ctx.enter_context(nc.semaphore(name))

        w_hi, w_lo = sb("w_hi", [P, WCOLS], F32R), sb("w_lo", [P, WCOLS], F32R)
        xt = [sb(f"xt{i}", [P, 2, KD, BT], F32R) for i in range(2)]
        ident, bias = sb("ident", [P, P]), sb("bias", [P, D])
        act_h = [sb(f"act_h{i}", [P, BT]) for i in range(2)]
        g_lo = [sb(f"g_lo{i}", [P, BT], F32R) for i in range(RING)]
        g_hi = [sb(f"g_hi{i}", [P, BT], F32R) for i in range(RING)]
        g_all = sb("g", [P, RING * BT])
        g = [g_all[:, i * BT:(i + 1) * BT] for i in range(RING)]
        xs = [sb(f"xs{i}", [P, D]) for i in range(TPP)]
        x1_all = sb("x1", [P, TPP * D])
        x1 = [x1_all[:, i * D:(i + 1) * D] for i in range(TPP)]
        fin = sb("fin", [P, TPB * D])
        xn = sb("xn", [P, D])
        row_hi, row_lo = sb("row_hi", [P, D], F32R), sb("row_lo", [P, D], F32R)
        nt = sb("nt", [P, 2, KD * P], F32R)
        qk = sb("qk", [P, 2 * D])
        vt = [sb(f"vt{i}", [P, D]) for i in range(2)]
        prod = [sb(f"prod{i}", [P, PROD]) for i in range(2)]
        score, att = sb("score", [P, D]), sb("att", [P, D])
        top, den, rden = sb("top", [P, HEADS]), sb("den", [P, HEADS]), sb("rden", [P, HEADS])
        stats = [sb(f"stats{i}", [P, 6]) for i in range(2)]
        mv = [sb(f"mv{i}", [P, 2]) for i in range(2)]
        var = [sb(f"var{i}", [P, 1]) for i in range(2)]
        rstd = [sb(f"rstd{i}", [P, 1]) for i in range(2)]
        minus = [sb(f"minus{i}", [P, 1]) for i in range(2)]
        shift = [sb(f"shift{i}", [P, 1]) for i in range(2)]
        neg_half, neg_one = sb("neg_half", [P, 1]), sb("neg_one", [P, 1])
        logit, sig = sb("logit", [P, TPB * E]), sb("sig", [P, TPB * E])
        gpick, epick = sb("gpick", [P, TPB, 10]), sb("epick", [P, TPB, 20])
        left = sb("left", [P, TPB, 20])
        best = sb("best", [P, TPB, 8])
        gsel, wsel = sb("gsel", [P, TPB * 4]), sb("wsel", [P, TPB * E])
        wden, hold = sb("wden", [P, TPB]), sb("hold", [P, 1])
        comb, comb_t = sb("comb", [P, E * TPB]), sb("comb_t", [E * TPB, P])

        h = [ps(f"h{i}") for i in range(RING)]
        y = ps("y")
        pa, pb = ps("pa"), ps("pb")

        consts = sem("consts")
        bias_in = sem("bias_in")
        piece_in = [sem(f"piece_in{i}") for i in range(4)]
        piece_hi, piece_lo = sem("piece_hi"), sem("piece_lo")
        x_in = [sem(f"x_in{i}") for i in range(TPP)]
        n_stats = [sem(f"n{i}_stats") for i in range(2)]
        n_mv = [sem(f"n{i}_mv") for i in range(2)]
        n_var = [sem(f"n{i}_var") for i in range(2)]
        n_rstd = [sem(f"n{i}_rstd") for i in range(2)]
        n_shift = [sem(f"n{i}_shift") for i in range(2)]
        n_out = [sem(f"n{i}_out") for i in range(2)]
        n_lo = [sem(f"n{i}_lo") for i in range(2)]
        n_ps = [sem(f"n{i}_ps") for i in range(2)]
        n_t = [sem(f"n{i}_t") for i in range(2)]
        qk_ps, v_ps, qk_sb, v_sb = sem("qk_ps"), sem("v_ps"), sem("qk_sb"), sem("v_sb")
        prod_done, red_done = sem("prod_done"), sem("red_done")
        top_done, shifted, exp_done = sem("top_done"), sem("shifted"), sem("exp_done")
        den_done, rden_done, att_done = sem("den_done"), sem("rden_done"), sem("att_done")
        at_hi, at_lo, at_ps, at_t = sem("at_hi"), sem("at_lo"), sem("at_ps"), sem("at_t")
        proj_ps, xb_done, x1_done = sem("proj_ps"), sem("xb_done"), sem("x1_done")
        gate_ps, logit_done, gate_exp = sem("gate_ps"), sem("logit_done"), sem("gate_exp")
        route, comb_done = sem("route"), sem("comb_done")
        comb_ps, comb_sb, comb_out = sem("comb_ps"), sem("comb_sb"), sem("comb_out")
        h_done, silu_done = sem("h_done"), sem("silu_done")
        cb_in = [sem(f"cb_in{i}") for i in range(RING)]
        weighted, g_done = sem("weighted"), sem("g_done")
        ghi_done, glo_done, down_done = sem("ghi_done"), sem("glo_done"), sem("down_done")
        y_done, y_out = sem("y_done"), sem("y_out")

        x_v = x.rearrange("(i j p) d -> i j p d", j=TPP, p=P)
        out_v = out.rearrange("(i e j p) d -> i e p j d", e=2, j=TPB, p=P)
        stage = [g_all[:, :STAGE], g_all[:, STAGE:2 * STAGE], fin[:], x1_all[:, STAGE:]]

        def piece_cols(k):
            return slice(k * STAGE, min((k + 1) * STAGE, WCOLS))

        def of_tiles(view, i, *place):
            if isinstance(i, int):
                return view[(i, *place)]
            part = view[(bass.ds(i, 1), *place)]
            return part.rearrange("o p d -> (o p) d" if len(part.shape) == 3 else "o p j d -> (o p) j d")

        def prologue_slots():
            per = -(-(PIECES - PIECES_ATT) // (3 * PHASE))
            for n, c in enumerate(range(-PHASE, NC)):
                first = PIECES_ATT + per * n
                yield c, range(min(first, PIECES), min(first + per, PIECES))

        def routed_upto(b, c):
            return b.count(EXC, c + 1 - SHC) if c >= SHC else b.count(EXC, min(c + 1, 0))

        block = ctx.enter_context(nc.Block())

        @block.sync
        def _(sp):
            def load_piece(k):
                wait(sp, piece_hi, k - 3)
                wait(sp, piece_lo, k - 3)
                cols = piece_cols(k)
                sp.dma_start(stage[k % 4][:, :cols.stop - cols.start], weights[:, cols]).then_inc(piece_in[k % 4], 16)

            def load_x(t):
                wait(sp, x1_done, t.done(back=TPP))
                i = t.block.of_pair(1, t.in_pair // TPP)
                sp.dma_start(xs[t.ring4][:], of_tiles(x_v, i, t.ring4)).then_inc(x_in[t.ring4], 16)

            def attention(b, c):
                if (st := slot_tiles(b, c)) is None:
                    return
                s, _, _, r = st
                ahead = Tile(b, r.offset + 1)
                if s == 0 and ahead.exists() and (ahead.number() is None or ahead.number() >= TPP):
                    load_x(ahead)

            def prologue(b):
                for n in range(TPP):
                    sp.dma_start(xs[n][:], x_v[0, n]).then_inc(x_in[n], 16)
                sp.dma_start(bias[:], b_out.partition_broadcast(P)).then_inc(bias_in, 16)
                for k in range(PIECES_ATT):
                    load_piece(k)
                for c, pieces in prologue_slots():
                    for k in pieces:
                        load_piece(k)
                    attention(b, c)

            def store_comb(b):
                if b.number() == 0:
                    sp.wait_ge(comb_sb, 1)
                else:
                    sp.wait_ge(glo_done, b.count(NC, 0))
                sp.dma_start(comb_dram[b.parity], comb_t[:]).then_inc(comb_out, 16)

            def store_out(b, back=1):
                sp.wait_ge(y_done, b.count(TPB, TPB - TPB * back))
                i = b.of_pair(1, (b.parity - back) // 2)
                sp.dma_start(of_tiles(out_v, i, (b.parity - back) % 2),
                             fin[:].rearrange("p (j d) -> p j d", j=TPB)).then_inc(y_out, 16)

            def load_weights_of_rows(b, n):
                for e, p0, p1 in SPANS[n]:
                    row = comb_dram[b.parity, e * TPB:(e + 1) * TPB, :].rearrange("j t -> (j t)")
                    sp.dma_start(g[n % RING][p0:p1, :], row.partition_broadcast(p1 - p0)).then_inc(cb_in[n % RING], 16)

            def slot(b, c):
                attention(b, c)
                if c == 0:
                    store_comb(b)
                if c == 1:
                    if b.number() == 0:
                        sp.wait_ge(piece_hi, PIECES)
                        sp.wait_ge(piece_lo, PIECES)
                    sp.wait_ge(comb_out, b.count(16, 16))
                    load_weights_of_rows(b, SHC)
                    load_weights_of_rows(b, SHC + 1)
                n = c + SHC
                if SHC + 1 < n < NC:
                    wait(sp, glo_done, b.count(NC, n - RING + 1))
                    load_weights_of_rows(b, n)
                if c == LAG + 1 and b.number() != 0:
                    store_out(b)

            def tail(b):
                store_out(b)
                sp.wait_ge(y_out, 16 * BLOCKS + 1)
                sp.wait_ge(comb_out, 16 * BLOCKS)

            run(sp, prologue, slot, tail, rates=(2, 4, 8, 32, 2 * EXC, 1))

        @block.scalar
        def _(act):
            def split_piece(k):
                cols = piece_cols(k)
                act.wait_ge(piece_in[k % 4], 16 * (k // 4 + 1))
                nc.scalar.activation(w_hi[:, cols], stage[k % 4][:, :cols.stop - cols.start],
                                     ACT.Copy).then_inc(piece_hi, 1)

            def norm_out(norm, t, src):
                act.wait_ge(n_shift[norm], t.done())
                for to in (xn, row_hi):
                    nc.scalar.activation(to[:], src[:], ACT.Identity, bias=shift[norm][:, 0:1],
                                         scale=rstd[norm][:, 0:1]).then_inc(n_out[norm], 1)

            def evacuate(ps_done, done, t):
                act.wait_ge(ps_done, t.done())
                nc.scalar.activation(nt[:], pa[:].rearrange("p (s c) -> p s c", s=2), ACT.Copy).then_inc(done, 1)

            def attention(b, c):
                if (st := slot_tiles(b, c)) is None:
                    return
                s, f, a, r = st
                if s == 1 and f.exists():
                    evacuate(at_ps, at_t, f)
                if s == 1 and r.exists():
                    norm_out(0, r, xs[r.ring4])
                if s == 4 and r.exists():
                    evacuate(n_ps[0], n_t[0], r)
                if s == 5 and f.exists():
                    norm_out(1, f, x1[f.ring4])
                if s == 5 and a.exists():
                    act.wait_ge(shifted, a.done())
                    nc.scalar.activation(score[:], score[:], ACT.Exp, scale=float(HD) ** -0.5).then_inc(exp_done, 1)
                if s == 6 and r.exists():
                    if a.exists():
                        act.wait_ge(prod_done, a.done(per_tile=2 * NG, part=NG))
                    qkv_out(r)
                if s == 7 and f.exists():
                    j = f.ring2
                    act.wait_ge(n_ps[1], f.done())
                    for part in range(2):
                        last = nc.scalar.activation(xt[1 - b.parity][:, part, :, j * P:(j + 1) * P],
                                                    pa[:, part * D:(part + 1) * D].rearrange("p (k t) -> p k t", k=KD), ACT.Copy)
                        last.then_inc(n_t[1], 1)
                if s == 8 and f.exists():
                    j = f.ring2
                    act.wait_ge(gate_ps, f.done())
                    nc.scalar.activation(logit[:, j * E:(j + 1) * E], pb[:, :E], ACT.Copy).then_inc(logit_done, 1)
                if c == PHASE + 8 and f.exists():
                    act.wait_ge(logit_done, f.done())
                    wait(act, comb_done, b.count(1, 1))
                    nc.scalar.activation(sig[:], logit[:], ACT.Exp, scale=-1.0).then_inc(gate_exp, 1)
                if s == 11 and a.exists():
                    act.wait_ge(att_done, a.done())
                    nc.scalar.activation(row_hi[:], att[:], ACT.Copy).then_inc(at_hi, 1)

            def qkv_out(t):
                act.wait_ge(qk_ps, t.done())
                nc.scalar.activation(qk[:], pb[:], ACT.Copy).then_inc(qk_sb, 1)
                act.wait_ge(v_ps, t.done())
                nc.scalar.activation(vt[t.ring2][:].rearrange("p (d h) -> p h d", h=HEADS),
                                     pa[:, :D].rearrange("p (h d) -> p h d", h=HEADS),
                                     ACT.Copy).then_inc(v_sb, 1)

            def comb_evacuated(b, c):
                if c == 0:
                    act.wait_ge(comb_ps, b.count(1, 1))
                    wait(act, comb_out, b.count(16, 0))
                    nc.scalar.activation(comb_t[:], pb[:E * TPB, :P], ACT.Copy).then_inc(comb_sb, 1)

            def prologue(b):
                first = Tile(b, 2)
                norm_out(0, first, xs[0])
                evacuate(n_ps[0], n_t[0], first)
                for k in range(PIECES_ATT):
                    split_piece(k)
                qkv_out(first)
                for c, pieces in prologue_slots():
                    for k in pieces:
                        split_piece(k)
                    attention(b, c)

            def slot(b, c):
                comb_evacuated(b, c)
                n, r = CHUNK_ROWS[c], c % RING
                act.wait_ge(h_done, b.count(NC, c + 1))
                nc.scalar.activation(act_h[(b.parity + c) % 2][:n], h[r][:n, :BT], ACT.Silu).then_inc(silu_done, 1)
                attention(b, c)
                ghi(b, c, 1)

            def ghi(b, c, lag):
                exists, n, r = behind(b, c, lag)
                if exists:
                    act.wait_ge(g_done, b.count(NC, c + 1 - lag))
                    nc.scalar.activation(g_hi[r][:n], g[r][:n], ACT.Copy).then_inc(ghi_done, 1)

            def tail(b):
                ghi(b, 0, 1)

            run(act, prologue, slot, tail)

        @block.gpsimd
        def _(pool):
            def split_piece(k):
                cols = piece_cols(k)
                n = cols.stop - cols.start
                pool.wait_ge(piece_hi, k + 1)
                nc.gpsimd.tensor_tensor(w_lo[:, cols], stage[k % 4][:, :n], w_hi[:, cols].bitcast(F32),
                                        ALU.subtract).then_inc(piece_lo, 1)

            def norm_factors(norm, t):
                pool.wait_ge(n_var[norm], t.done())
                nc.gpsimd.tensor_tensor(rstd[norm][:], var[norm][:], neg_half[:], ALU.pow).then_inc(n_rstd[norm], 1)
                nc.gpsimd.tensor_tensor(minus[norm][:], mv[norm][:, 0:1], neg_one[:], ALU.mult).then_inc(n_rstd[norm], 1)
                pool.wait_ge(n_rstd[norm], t.done(per_tile=2))
                nc.gpsimd.tensor_tensor(shift[norm][:], minus[norm][:], rstd[norm][:], ALU.mult).then_inc(n_shift[norm], 1)

            def x_plus_bias(t):
                pool.wait_ge(n_out[0], t.done(per_tile=2))
                nc.gpsimd.tensor_tensor(xs[t.ring4][:], xs[t.ring4][:], bias[:], ALU.add).then_inc(xb_done, 1)

            def lo_of(src, hi_done, done, count, t):
                pool.wait_ge(hi_done, count)
                nc.gpsimd.tensor_tensor(row_lo[:], src[:], row_hi[:].bitcast(F32), ALU.subtract).then_inc(done, 1)

            def attention(b, c):
                if (st := slot_tiles(b, c)) is None:
                    return
                s, f, a, r = st
                if s == 0 and f.exists():
                    lo_of(att, at_hi, at_lo, f.done(), f)
                if s == 1 and r.exists():
                    norm_factors(0, r)
                if s == 3 and r.exists():
                    lo_of(xn, n_out[0], n_lo[0], r.done(per_tile=2), r)
                if s == 4 and f.exists():
                    norm_factors(1, f)
                if s == 5 and a.exists():
                    s3 = score[:].rearrange("p (h g) -> p h g", h=HEADS)
                    pool.wait_ge(top_done, a.done())
                    nc.gpsimd.tensor_tensor(s3, s3, top[:, :, None].broadcast_to([P, HEADS, HEADS]),
                                            ALU.subtract).then_inc(shifted, 1)
                if s == 6 and f.exists():
                    lo_of(xn, n_out[1], n_lo[1], f.done(per_tile=2), f)
                if s == 8 and r.exists():
                    x_plus_bias(r)
                if s == 11 and a.exists():
                    a3 = att[:].rearrange("p (h d) -> p h d", h=HEADS)
                    pool.wait_ge(red_done, a.done(per_tile=2 * NG))
                    pool.wait_ge(rden_done, a.done())
                    nc.gpsimd.tensor_tensor(a3, a3, rden[:, :, None].broadcast_to([P, HEADS, HD]),
                                            ALU.mult).then_inc(att_done, 1)

            def prologue(b):
                nc.gpsimd.memset(neg_half[:], -0.5).then_inc(consts, 1)
                nc.gpsimd.memset(neg_one[:], -1.0).then_inc(consts, 1)
                nc.gpsimd.memset(ident[:], 0.0).then_inc(consts, 1)
                pool.wait_ge(consts, 3)
                pool.affine_select(out=ident[:], in_=ident[:], compare_op=ALU.not_equal, fill=1.0, base=0,
                                   pattern=[[-1, P]], channel_multiplier=1).then_inc(consts, 1)
                first = Tile(b, 2)
                norm_factors(0, first)
                lo_of(xn, n_out[0], n_lo[0], first.done(per_tile=2), first)
                for k in range(PIECES_ATT):
                    split_piece(k)
                pool.wait_ge(bias_in, 16)
                x_plus_bias(first)
                for c, pieces in prologue_slots():
                    attention(b, c)
                    for k in pieces:
                        split_piece(k)

            def slot(b, c):
                attention(b, c)
                if c >= SHC:
                    r = c % RING
                    pool.wait_ge(silu_done, b.count(NC, c + 1))
                    pool.wait_ge(cb_in[r], b.count(16 * CB_ALL[r], 16 * CB_UPTO[c]))
                    nc.gpsimd.tensor_tensor(g[r], act_h[(b.parity + c) % 2][:], g[r], ALU.mult).then_inc(weighted, 1)
                glo(b, c, 1)

            def glo(b, c, lag):
                exists, n, r = behind(b, c, lag)
                if exists:
                    pool.wait_ge(ghi_done, b.count(NC, c + 1 - lag))
                    nc.gpsimd.tensor_tensor(g_lo[r][:n], g[r][:n], g_hi[r][:n].bitcast(F32),
                                            ALU.subtract).then_inc(glo_done, 1)

            def tail(b):
                glo(b, 0, 1)

            run(pool, prologue, slot, tail)

        @block.vector
        def _(dve):
            vec = nc.vector

            def carry_wait():
                vec.memset(hold[:], 0.0)

            def norm_stats(norm, t, src):
                vec.bn_stats(stats[norm][:], src[:]).then_inc(n_stats[norm], 1)

            def norm_var(norm, t):
                dve.wait_ge(n_stats[norm], t.done())
                carry_wait()
                vec.bn_aggr(mv[norm][:], stats[norm][:]).then_inc(n_mv[norm], 1)
                dve.wait_ge(n_mv[norm], t.done())
                vec.tensor_scalar(var[norm][:], mv[norm][:, 1:2], EPS, None, ALU.add).then_inc(n_var[norm], 1)

            def product(t, n):
                i = n % NG
                heads = slice(i * GROUP * HD, (i + 1) * GROUP * HD)
                if n == 0:
                    dve.wait_ge(qk_sb, t.done())
                if n == NG:
                    dve.wait_ge(exp_done, t.done())
                    dve.wait_ge(v_sb, t.done())
                wait(dve, red_done, t.done(per_tile=2 * NG, part=2 * NG + 1 - n))
                left = (qk[:, heads] if n < NG else score[:, heads]).rearrange("p (h d) -> p h d", h=GROUP)
                right = (qk[:, D:] if n < NG else vt[t.ring2][:]).rearrange("p (h d) -> p h d", h=HEADS)
                shape = [P, GROUP, HEADS, HD]
                vec.tensor_tensor(prod[n % 2][:].rearrange("p (g h d) -> p g h d", g=GROUP, h=HEADS),
                                  left[:, :, None, :].broadcast_to(shape), right[:, None, :, :].broadcast_to(shape),
                                  ALU.mult).then_inc(prod_done, 1)

            def reduced(t, n):
                i = n % NG
                to = (score if n < NG else att)[:, i * GROUP * HD:(i + 1) * GROUP * HD]
                dve.wait_ge(prod_done, t.done(per_tile=2 * NG, part=2 * NG - 1 - n))
                if n == NG:
                    wait(dve, at_lo, t.done(back=1))
                vec.tensor_reduce(to, prod[n % 2][:].rearrange("p (x d) -> p x d", d=HD), AX.X, ALU.add).then_inc(red_done, 1)

            def maximum(t):
                dve.wait_ge(red_done, t.done(per_tile=2 * NG, part=NG))
                vec.tensor_reduce(top[:], score[:].rearrange("p (h g) -> p h g", h=HEADS), AX.X, ALU.max).then_inc(top_done, 1)

            def denominator(t):
                dve.wait_ge(exp_done, t.done())
                vec.tensor_reduce(den[:], score[:].rearrange("p (h g) -> p h g", h=HEADS), AX.X,
                                  ALU.add).then_inc(den_done, 1)

            def inverse_denominator(t):
                dve.wait_ge(den_done, t.done())
                vec.reciprocal(rden[:], den[:]).then_inc(rden_done, 1)

            def residual(t):
                dve.wait_ge(proj_ps, t.done())
                dve.wait_ge(xb_done, t.done())
                vec.tensor_tensor(x1[t.ring4], pb[:, :D], xs[t.ring4][:], ALU.add).then_inc(x1_done, 1)

            def attention_before(b, c):
                if (st := slot_tiles(b, c)) is None:
                    return
                s, f, a, r = st
                if s == 0 and r.exists():
                    dve.wait_ge(x_in[r.ring4], r.dma())
                    norm_stats(0, r, xs[r.ring4])
                if s == 3 and f.exists():
                    if c == 3:
                        wait(dve, y_done, b.count(TPB, 0))
                    residual(f)
                    dve.wait_ge(x1_done, f.done())
                    norm_stats(1, f, x1[f.ring4])
                if a.exists():
                    if s == 0:
                        product(a, 0)
                    if s == 1:
                        reduced(a, 0)
                    if s == 2:
                        reduced(a, 1)
                    if s == 4:
                        reduced(a, 2)
                    if s == 7:
                        product(a, 5)
                    if s == 8:
                        product(a, 6)
                    if s == 9:
                        product(a, 7)
                    if s == 10:
                        reduced(a, 7)
                if PHASE + 10 <= c < PHASE + 12 and f.exists():
                    routing(b, c - PHASE - 9)

            def attention_behind(b, c):
                if (st := slot_tiles(b, c)) is None:
                    return
                s, f, a, r = st
                if s == 0 and r.exists():
                    norm_var(0, r)
                if s == 3 and f.exists():
                    norm_var(1, f)
                if c == PHASE + 9 and f.exists():
                    routing(b, 0)
                if a.exists():
                    if s == 0:
                        product(a, 1)
                    if s == 1:
                        product(a, 2)
                    if s == 2:
                        product(a, 3)
                    if s == 4:
                        reduced(a, 3)
                        maximum(a)
                    if s == 6:
                        denominator(a)
                        product(a, 4)
                        inverse_denominator(a)
                    if s == 7:
                        reduced(a, 4)
                    if s == 8:
                        reduced(a, 5)
                    if s == 9:
                        reduced(a, 6)

            ROUTE_AT = (0, 5, 9)
            ROUTE = 14

            def routing(b, part):
                step = [ROUTE_AT[part]]

                def then(ins):
                    step[0] += 1
                    ins.then_inc(route, 1)

                def after_last():
                    dve.wait_ge(route, b.count(ROUTE, ROUTE + step[0]))

                w3 = wsel[:].rearrange("p (j e) -> p j e", j=TPB)
                if part == 0:
                    dve.wait_ge(gate_exp, b.count(1, 2))
                    then(vec.tensor_scalar(sig[:], sig[:], 1.0, None, ALU.add))
                    after_last()
                    then(vec.reciprocal(sig[:], sig[:]))
                    after_last()
                    then(vec.tensor_reduce(gpick[:, :, 0:4], sig[:].rearrange("p (j g e) -> p j g e", j=TPB, g=4), AX.X, ALU.max))
                    after_last()
                    carry_wait()
                    for j in range(TPB):
                        last = vec.max(best[:, j], gpick[:, j])
                    then(last)
                    after_last()
                    then(vec.memset(best[:, :, 2:], -1.0))
                if part == 1:
                    after_last()
                    carry_wait()
                    for j in range(TPB):
                        last = vec.match_replace(left[:, j, 0:10], best[:, j], gpick[:, j], -9.0)
                    then(last)
                    after_last()
                    then(vec.tensor_scalar(gsel[:].rearrange("p (j g) -> p j g", j=TPB), left[:, :, 0:4], -2.0, None, ALU.is_lt))
                    after_last()
                    then(vec.tensor_tensor(epick[:, :, 0:E].rearrange("p j (g e) -> p j g e", g=4),
                                           sig[:].rearrange("p (j g e) -> p j g e", j=TPB, g=4),
                                           gsel[:].rearrange("p (j g) -> p j g", j=TPB)[:, :, :, None].broadcast_to([P, TPB, 4, 4]),
                                           ALU.mult))
                    after_last()
                    carry_wait()
                    for j in range(TPB):
                        last = vec.max(best[:, j], epick[:, j])
                    then(last)
                if part == 2:
                    after_last()
                    then(vec.memset(best[:, :, 4:], -1.0))
                    after_last()
                    carry_wait()
                    for j in range(TPB):
                        last = vec.match_replace(left[:, j], best[:, j], epick[:, j], -9.0)
                    then(last)
                    after_last()
                    then(vec.scalar_tensor_tensor(w3, left[:, :, 0:E], -2.0, sig[:].rearrange("p (j e) -> p j e", j=TPB),
                                                  ALU.is_lt, ALU.mult))
                    after_last()
                    then(vec.tensor_reduce(wden[:], w3, AX.X, ALU.add))
                    after_last()
                    then(vec.reciprocal(wden[:], wden[:]))
                    after_last()
                    wait(dve, comb_ps, b.count(1, 1))
                    vec.tensor_tensor(comb[:].rearrange("p (e j) -> p j e", j=TPB), w3,
                                      wden[:, :, None].broadcast_to([P, TPB, E]), ALU.mult).then_inc(comb_done, 1)
                assert step[0] == (ROUTE_AT + (ROUTE,))[part + 1]

            def prologue(b):
                vec.memset(gpick[:, :, 4:], -1.0)
                vec.memset(epick[:, :, E:], -1.0).then_inc(y_out, 1)
                dve.wait_ge(y_out, 1)
                first = Tile(b, 2)
                dve.wait_ge(x_in[0], 16)
                norm_stats(0, first, xs[0])
                norm_var(0, first)
                for c, _ in prologue_slots():
                    attention_before(b, c)
                    attention_behind(b, c)

            def finish(b):
                dve.wait_ge(down_done, b.count(NC, 0))
                dve.wait_ge(y_out, b.count(16, 1 - 16))
                for j in range(TPB):
                    at = slice(j * D, (j + 1) * D)
                    vec.tensor_tensor(fin[:, at], y[:, at], x1[(TPB * (1 - b.parity) + j) % TPP], ALU.add).then_inc(y_done, 1)

            def gate(b, c, lag):
                exists, n, r = behind(b, c, lag)
                if exists:
                    dve.wait_ge(h_done, b.count(NC, c + 1 - lag))
                    left = g[r]
                    if 0 <= c - lag < SHC:
                        dve.wait_ge(silu_done, b.count(NC, c + 1 - lag))
                        wait(dve, glo_done, b.count(NC, c + 1 - lag - RING))
                        left = act_h[(b.parity + c - lag) % 2]
                    else:
                        dve.wait_ge(weighted, routed_upto(b, c - lag))
                    vec.tensor_tensor(g[r][:n], left[:n], h[r][:n, BT:], ALU.mult).then_inc(g_done, 1)

            def slot(b, c):
                if c == LAG and b.number() != 0:
                    finish(b)
                if c == LAG and b.number() == 0:
                    dve.wait_ge(piece_lo, PIECES)
                attention_before(b, c)
                gate(b, c, 1)
                attention_behind(b, c)

            def tail(b):
                gate(b, 0, 1)
                finish(b)

            run(dve, prologue, slot, tail)

        @block.tensor
        def _(pe):
            mm = nc.tensor.matmul

            def product(to, left, right, **kw):
                for n, (lp, rp) in enumerate(((0, 0), (0, 1), (1, 0))):
                    for k in range(KD):
                        last = mm(to, left(lp, k), right(rp, k), start=(n == 0 and k == 0), stop=(n == 2 and k == KD - 1), **kw)
                return last

            def weight(at, width, first, count):
                return lambda part, k: (w_hi, w_lo)[part][:, at + k * width + first:at + k * width + first + count]

            def of_nt(part, k):
                return nt[:, part, k * P:(k + 1) * P]

            def transposes():
                for part, src in enumerate((row_hi, row_lo)):
                    for k in range(KD):
                        last = nc.tensor.transpose(pa[:, part * D + k * P:part * D + (k + 1) * P],
                                                   src[:, k * P:(k + 1) * P].bitcast(F32), ident[:])
                return last

            def n1_transposed(t):
                pe.wait_ge(n_lo[0], t.done())
                transposes().then_inc(n_ps[0], 1)

            def qkv(t):
                pe.wait_ge(n_t[0], t.done())
                product(pb[:], of_nt, weight(AT_QKV, 3 * D, 0, 2 * D)).then_inc(qk_ps, 1)
                product(pa[:, :D], of_nt, weight(AT_QKV, 3 * D, 2 * D, D)).then_inc(v_ps, 1)

            def attention(b, c):
                if (st := slot_tiles(b, c)) is None:
                    return
                s, f, a, r = st
                before = Tile(b, f.offset - 1)
                if s == 1 and f.exists():
                    pe.wait_ge(at_lo, f.done())
                    if a.exists() and not before.exists():
                        pe.wait_ge(v_sb, a.done())
                    transposes().then_inc(at_ps, 1)
                if s == 2 and f.exists():
                    if c == 2 and b.number() != -1:
                        pe.wait_ge(comb_sb, b.count(1, 1))
                    elif before.exists():
                        pe.wait_ge(logit_done, before.done())
                    elif a.exists():
                        pe.wait_ge(qk_sb, a.done())
                    pe.wait_ge(at_t, f.done())
                    product(pb[:, :D], of_nt, weight(AT_WO, D, 0, D)).then_inc(proj_ps, 1)
                if s == 4 and r.exists():
                    if not f.exists():
                        wait(pe, v_sb, r.done(back=1))
                    n1_transposed(r)
                if s == 5 and r.exists():
                    if f.exists():
                        pe.wait_ge(x1_done, f.done())
                    else:
                        wait(pe, qk_sb, r.done(back=1))
                    qkv(r)
                if s == 7 and f.exists():
                    if r.exists():
                        pe.wait_ge(v_sb, r.done())
                    pe.wait_ge(n_lo[1], f.done())
                    transposes().then_inc(n_ps[1], 1)
                if s == 8 and f.exists():
                    j, par = f.ring2, 1 - b.parity
                    pe.wait_ge(*((qk_sb, r.done()) if r.exists() else (x1_done, f.done())))
                    pe.wait_ge(n_t[1], f.done(per_tile=2))
                    product(pb[:, :E], lambda part, k: xt[par][:, part, k, j * P:(j + 1) * P],
                            weight(AT_GATE, E, 0, E)).then_inc(gate_ps, 1)

            def comb_transposed(b, c):
                if c == NC - 1:
                    pe.wait_ge(comb_done, b.count(1, 2))
                    mm(pb[:E * TPB, :P], comb[:], ident[:], start=True, stop=True).then_inc(comb_ps, 1)

            def prologue(b):
                first = Tile(b, 2)
                pe.wait_ge(consts, 4)
                n1_transposed(first)
                pe.wait_ge(piece_lo, PIECES_ATT)
                qkv(first)
                for c, _ in prologue_slots():
                    attention(b, c)
                    comb_transposed(b, c)

            def rows(b, c):
                n, at, r, par = CHUNK_ROWS[c], AT_CHUNK[c], c % RING, b.parity
                if b.number() == 0 and c < LAG:
                    pe.wait_ge(piece_lo, pieces_until(AT_CHUNK[c + 1]))
                if b.number() == 0 and c == LAG:
                    pe.wait_ge(piece_lo, PIECES)
                if c == 0:
                    pe.wait_ge(n_t[1], b.count(2 * TPB, 2 * TPB))
                wait(pe, g_done, b.count(NC, c + 1 - RING))
                for to, w_at in ((h[r][:n, :BT], at), (h[r][:n, BT:], at + KD * n)):
                    last = product(to, weight(w_at, n, 0, n), lambda part, k: xt[par][:, part, k, :])
                last.then_inc(h_done, 1)

            def down(b, c, lag):
                exists, n, r = behind(b, c, lag)
                if not exists:
                    return
                chunk = (c - lag) % NC
                pe.wait_ge(glo_done, b.count(NC, c + 1 - lag))
                if chunk == 0:
                    wait(pe, y_done, b.count(TPB, 0))
                w = slice(AT_CHUNK[chunk + 1] - D, AT_CHUNK[chunk + 1])
                for j in range(TPB):
                    tok = slice(j * P, (j + 1) * P)
                    for m, (gp, wp) in enumerate(((g_hi[r], w_hi), (g_hi[r], w_lo), (g_lo[r], w_hi))):
                        last = mm(y[:, j * D:(j + 1) * D], gp[:n, tok], wp[:n, w],
                                  start=(chunk == 0 and j == 0 and m == 0),
                                  stop=(chunk == NC - 1 and j == TPB - 1 and m == 2), skip_group_check=True)
                last.then_inc(down_done, 1)

            def slot(b, c):
                rows(b, c)
                attention(b, c)
                down(b, c, LAG)
                if b.number() != BLOCKS - 1:
                    comb_transposed(b, c)

            def tail(b):
                for c in range(LAG):
                    down(b, c, LAG)

            run(pe, prologue, slot, tail)


def kernel(L0_attn_x, L0_attn_W_qkv, L0_attn_W_out, L0_attn_b_out, L0_ffn_gate_w, L0_ffn_W1, L0_ffn_W2,
           L0_ffn_W3, L0_ffn_Ws1, L0_ffn_Ws2, L0_ffn_Ws3):
    import numpy as np
    import concourse.bacc as bacc
    from concourse.bass_utils import run_bass_kernel_spmd

    def by_contraction(w):
        w = np.asarray(w)
        return w.reshape(KD, P, w.shape[1]).transpose(1, 0, 2).reshape(P, -1)

    w1 = np.concatenate([np.asarray(L0_ffn_Ws1), np.asarray(L0_ffn_W1).reshape(E * I, D)])
    w3 = np.concatenate([np.asarray(L0_ffn_Ws3), np.asarray(L0_ffn_W3).reshape(E * I, D)])
    w2 = np.concatenate([np.asarray(L0_ffn_Ws2).T, np.asarray(L0_ffn_W2).transpose(0, 2, 1).reshape(E * I, D)])
    parts = [by_contraction(L0_attn_W_qkv), by_contraction(L0_attn_W_out), by_contraction(np.asarray(L0_ffn_gate_w).T)]
    first = 0
    for rows in CHUNK_ROWS:
        chunk = slice(first, first + rows)
        pad = np.zeros((P - rows, D), w2.dtype)
        parts += [by_contraction(w1[chunk].T), by_contraction(w3[chunk].T), np.concatenate([w2[chunk], pad])]
        first += rows
    packed = np.concatenate(parts, axis=1)
    assert packed.shape == (P, WCOLS)
    arrays = {
        "x": np.ascontiguousarray(np.asarray(L0_attn_x).reshape(T, D)),
        "weights": np.ascontiguousarray(packed),
        "b_out": np.ascontiguousarray(np.asarray(L0_attn_b_out)),
    }
    nc = bacc.Bacc("TRN2", target_bir_lowering=False, num_devices=1, dynamic_dma_scratch_size=512)
    ins = [nc.dram_tensor(n, a.shape, mybir.dt.from_np(a.dtype), kind="ExternalInput").ap() for n, a in arrays.items()]
    comb = nc.dram_tensor("comb_by_expert", (2, E * TPB, P), F32, kind="Internal").ap()
    out = nc.dram_tensor("out", (T, D), F32, kind="ExternalOutput").ap()
    build(nc, *ins, comb, out)
    r = run_bass_kernel_spmd(nc, [arrays], core_ids=[0])
    return r.results[0]["out"].reshape(np.asarray(L0_attn_x).shape)
```

```python
from contextlib import ExitStack

import concourse.bass as bass
from concourse import mybir

F32 = mybir.dt.float32
F32R = mybir.dt.float32r
ALU = mybir.AluOpType
ACT = mybir.ActivationFunctionType
AX = mybir.AxisListType

P = 128
T, D = 4096, 256
KD = D // P
HEADS, HD = 16, 16
E, I, SH = 16, 176, 352
TILES, TPB = T // P, 2
BLOCKS, BT = TILES // TPB, TPB * P
TPP = 2 * TPB
SHC = -(-SH // P)
EXC = E * I // P
NC = SHC + EXC
RING = 5
EPS = 1e-5
PHASE = 12
GROUP = 4
NG = HEADS // GROUP
PROD = GROUP * HEADS * HD

CHUNK_ROWS = [min(P, SH - c * P) for c in range(SHC)] + [P] * EXC

AT_QKV = 0
AT_WO = AT_QKV + KD * 3 * D
AT_GATE = AT_WO + KD * D
AT_CHUNK = [AT_GATE + KD * E]
for _rows in CHUNK_ROWS:
    AT_CHUNK.append(AT_CHUNK[-1] + 2 * KD * _rows + D)
WCOLS = AT_CHUNK[-1]
STAGE = 512


def pieces_until(col):
    return -(-col // STAGE)


PIECES = pieces_until(WCOLS)
PIECES_QKV = pieces_until(AT_WO)
PIECES_ATT = pieces_until(AT_CHUNK[0])

PIECES_IN_SLOT = (0, 1, 1, 1, 0, 0, 2, 2, 2, 2, 1, 0)
PROLOGUE, _next = [], PIECES_ATT
for _c in range(-PHASE, NC):
    _count = PIECES_IN_SLOT[_c % PHASE] if _c < 2 * PHASE else 1
    PROLOGUE.append((_c, range(_next, min(_next + _count, PIECES))))
    _next = min(_next + _count, PIECES)
assert _next == PIECES

SPANS = {}
for _n in range(EXC):
    _r, _spans = _n * P, []
    while _r < (_n + 1) * P:
        _end = min((_n + 1) * P, (_r // I + 1) * I)
        _spans.append((_r // I, _r - _n * P, _end - _n * P))
        _r = _end
    SPANS[SHC + _n] = _spans
CB_UPTO = {c: sum(len(SPANS[m]) for m in SPANS if m % RING == c % RING and m <= c) for c in SPANS}
CB_ALL = [sum(len(SPANS[m]) for m in SPANS if m % RING == r) for r in range(RING)]

LAG = 4
LAST = 4
PEEL = RING


class Block:

    def __init__(self, eng, i, parity, bases=None, pairs_on=0):
        self.eng, self.i, self.parity, self.pairs_on = eng, i, parity, pairs_on
        self.bases = {} if bases is None else bases

    def next(self):
        if isinstance(self.i, int):
            n = 2 * self.i + self.parity + 1
            return Block(self.eng, n // 2, n % 2)
        return Block(self.eng, self.i, 1 - self.parity, self.bases, self.pairs_on + self.parity)

    def of_pair(self, per_pair, offset):
        if isinstance(self.i, int):
            return per_pair * self.i + offset
        if per_pair not in self.bases:
            self.bases[per_pair] = self.eng.snap(self.i * per_pair)
        return self.bases[per_pair] + (offset + per_pair * self.pairs_on)

    def count(self, per_block, offset):
        return self.of_pair(2 * per_block, offset + per_block * self.parity)

    def number(self):
        return 2 * self.i + self.parity if isinstance(self.i, int) else None


class Tile:

    def __init__(self, block, offset):
        self.block, self.offset = block, offset
        self.in_pair = TPB * block.parity + offset
        self.ring4, self.ring2 = self.in_pair % TPP, offset % 2

    def done(self, back=0, per_tile=1, part=0):
        return self.block.count(TPB * per_tile, per_tile * (self.offset + 1 - back) - part)

    def dma(self):
        return self.block.of_pair(16, 16 * (self.in_pair // TPP + 1))

    def number(self):
        n = self.block.number()
        return None if n is None else TPB * n + self.offset

    def exists(self):
        return self.number() is None or 0 <= self.number() < TILES


def wait(eng, sem, value):
    if not isinstance(value, int) or value > 0:
        eng.wait_ge(sem, value)


def slot_tiles(b, c):
    if c >= 2 * PHASE:
        return None
    p = c // PHASE
    return c % PHASE, Tile(b, 2 + p), Tile(b, 3 + p), Tile(b, 4 + p)


def behind(b, c, lag):
    return b.number() != 0 or c >= lag, CHUNK_ROWS[(c - lag) % NC], (c - lag) % RING


def run(eng, prologue, slot, tail, rates=()):
    prologue(Block(eng, -1, 1))
    for c in range(PEEL):
        slot(Block(eng, 0, 0), c)
    with eng.Fori(0, (BLOCKS - LAST) // 2) as i:
        b = Block(eng, i, 0)
        for rate in rates:
            b.of_pair(rate, 0)
        for _ in range(2):
            for c in range(PEEL, NC):
                slot(b, c)
            b = b.next()
            for c in range(PEEL):
                slot(b, c)
    for n in range(BLOCKS - LAST, BLOCKS):
        b = Block(eng, n // 2, n % 2)
        for c in range(PEEL, NC):
            slot(b, c)
        if n < BLOCKS - 1:
            for c in range(PEEL):
                slot(b.next(), c)
    tail(Block(eng, BLOCKS // 2, 0))


def build(nc, x, weights, b_out, comb_dram, out):
    with ExitStack() as ctx:
        def sb(name, shape, dt=F32):
            return ctx.enter_context(nc.sbuf_tensor(name, shape, dt))

        def ps(name):
            return ctx.enter_context(nc.psum_tensor(name, [P, 512], F32))

        def sem(name):
            return ctx.enter_context(nc.semaphore(name))

        w_hi, w_lo = sb("w_hi", [P, WCOLS], F32R), sb("w_lo", [P, WCOLS], F32R)
        xt = [sb(f"xt{i}", [P, 2, KD, BT], F32R) for i in range(2)]
        ident, bias = sb("ident", [P, P]), sb("bias", [P, D])
        act_h = [sb(f"act_h{i}", [P, BT]) for i in range(2)]
        g_lo = [sb(f"g_lo{i}", [P, BT], F32R) for i in range(RING)]
        g_hi = [sb(f"g_hi{i}", [P, BT], F32R) for i in range(RING)]
        g_all = sb("g", [P, RING * BT])
        g = [g_all[:, i * BT:(i + 1) * BT] for i in range(RING)]
        xs = [sb(f"xs{i}", [P, D]) for i in range(TPP)]
        x1_all = sb("x1", [P, TPP * D])
        x1 = [x1_all[:, i * D:(i + 1) * D] for i in range(TPP)]
        fin = sb("fin", [P, TPB * D])
        xn = sb("xn", [P, D])
        nt = sb("nt", [P, 2, KD * P], F32R)
        qk = sb("qk", [P, 2 * D])
        vt = [sb(f"vt{i}", [P, D]) for i in range(2)]
        prod = [sb(f"prod{i}", [P, PROD]) for i in range(2)]
        score, att = sb("score", [P, D]), sb("att", [P, D])
        top, den, rden = sb("top", [P, HEADS]), sb("den", [P, HEADS]), sb("rden", [P, HEADS])
        stats = [sb(f"stats{i}", [P, 6]) for i in range(2)]
        mv = [sb(f"mv{i}", [P, 2]) for i in range(2)]
        var = [sb(f"var{i}", [P, 1]) for i in range(2)]
        rstd = [sb(f"rstd{i}", [P, 1]) for i in range(2)]
        minus = [sb(f"minus{i}", [P, 1]) for i in range(2)]
        shift = [sb(f"shift{i}", [P, 1]) for i in range(2)]
        neg_half, neg_one = sb("neg_half", [P, 1]), sb("neg_one", [P, 1])
        logit, sig = sb("logit", [P, TPB * E]), sb("sig", [P, TPB * E])
        gpick, epick = sb("gpick", [P, TPB, 10]), sb("epick", [P, TPB, 20])
        left = sb("left", [P, TPB, 20])
        best = sb("best", [P, TPB, 8])
        gsel, wsel = sb("gsel", [P, TPB * 4]), sb("wsel", [P, TPB * E])
        wden, hold = sb("wden", [P, TPB]), sb("hold", [P, 1])
        comb, comb_t = sb("comb", [P, E * TPB]), sb("comb_t", [E * TPB, P])

        h = [ps(f"h{i}") for i in range(RING)]
        y = ps("y")
        pa, pb = ps("pa"), ps("pb")

        consts = sem("consts")
        bias_in = sem("bias_in")
        piece_in = [sem(f"piece_in{i}") for i in range(4)]
        piece_hi = sem("piece_hi")
        piece_lo, piece_lo_v = sem("piece_lo"), sem("piece_lo_v")
        x_in = [sem(f"x_in{i}") for i in range(TPP)]
        n_stats = [sem(f"n{i}_stats") for i in range(2)]
        n_mv = [sem(f"n{i}_mv") for i in range(2)]
        n_var = [sem(f"n{i}_var") for i in range(2)]
        n_rstd = [sem(f"n{i}_rstd") for i in range(2)]
        n_shift = [sem(f"n{i}_shift") for i in range(2)]
        n_out = [sem(f"n{i}_out") for i in range(2)]
        n_ps = [sem(f"n{i}_ps") for i in range(2)]
        n_hi = [sem(f"n{i}_hi") for i in range(2)]
        n_lo = [sem(f"n{i}_lo") for i in range(2)]
        qk_ps, v_ps, qk_sb, v_sb = sem("qk_ps"), sem("v_ps"), sem("qk_sb"), sem("v_sb")
        prod_done, red_done = sem("prod_done"), sem("red_done")
        top_done, shifted, exp_done = sem("top_done"), sem("shifted"), sem("exp_done")
        den_done, rden_done, att_done = sem("den_done"), sem("rden_done"), sem("att_done")
        at_ps, at_hi, at_lo = sem("at_ps"), sem("at_hi"), sem("at_lo")
        proj_ps, xb_done, x1_done = sem("proj_ps"), sem("xb_done"), sem("x1_done")
        gate_ps, logit_done, gate_exp = sem("gate_ps"), sem("logit_done"), sem("gate_exp")
        route, comb_done = sem("route"), sem("comb_done")
        comb_ps, comb_sb, comb_out = sem("comb_ps"), sem("comb_sb"), sem("comb_out")
        h_done, silu_done = sem("h_done"), sem("silu_done")
        cb_in = [sem(f"cb_in{i}") for i in range(RING)]
        weighted, g_done = sem("weighted"), sem("g_done")
        ghi_done, glo_done, down_done = sem("ghi_done"), sem("glo_done"), sem("down_done")
        y_done, y_out = sem("y_done"), sem("y_out")

        x_v = x.rearrange("(i j p) d -> i j p d", j=TPP, p=P)
        out_v = out.rearrange("(i e j p) d -> i e p j d", e=2, j=TPB, p=P)
        stage = [g_all[:, :STAGE], g_all[:, STAGE:2 * STAGE], fin[:], x1_all[:, STAGE:]]

        def piece_cols(k):
            return slice(k * STAGE, min((k + 1) * STAGE, WCOLS))

        def of_tiles(view, i, *place):
            if isinstance(i, int):
                return view[(i, *place)]
            part = view[(bass.ds(i, 1), *place)]
            return part.rearrange("o p d -> (o p) d" if len(part.shape) == 3 else "o p j d -> (o p) j d")

        def wait_split(eng, until):
            on_vector = min(until, PIECES_QKV)
            wait(eng, piece_hi, until)
            wait(eng, piece_lo, until - on_vector)
            wait(eng, piece_lo_v, on_vector)

        def routed_upto(b, c):
            return b.count(EXC, c + 1 - SHC) if c >= SHC else b.count(EXC, min(c + 1, 0))

        block = ctx.enter_context(nc.Block())

        @block.sync
        def _(sp):
            def load_piece(k):
                wait_split(sp, max(k - 3, 0))
                cols = piece_cols(k)
                sp.dma_start(stage[k % 4][:, :cols.stop - cols.start], weights[:, cols]).then_inc(piece_in[k % 4], 16)

            def load_x(t):
                wait(sp, x1_done, t.done(back=TPP))
                i = t.block.of_pair(1, t.in_pair // TPP)
                sp.dma_start(xs[t.ring4][:], of_tiles(x_v, i, t.ring4)).then_inc(x_in[t.ring4], 16)

            def attention(b, c):
                if (st := slot_tiles(b, c)) is None:
                    return
                s, _, _, r = st
                ahead = Tile(b, r.offset + 1)
                if s == 0 and ahead.exists() and (ahead.number() is None or ahead.number() >= TPP):
                    load_x(ahead)

            def prologue(b):
                sp.dma_start(xs[0][:], x_v[0, 0]).then_inc(x_in[0], 16)
                for k in range(PIECES_QKV):
                    load_piece(k)
                sp.dma_start(bias[:], b_out.partition_broadcast(P)).then_inc(bias_in, 16)
                for n in range(1, TPP):
                    sp.dma_start(xs[n][:], x_v[0, n]).then_inc(x_in[n], 16)
                for k in range(PIECES_QKV, PIECES_ATT):
                    load_piece(k)
                for c, pieces in PROLOGUE:
                    for k in pieces:
                        load_piece(k)
                    attention(b, c)

            def store_comb(b):
                sp.wait_ge(comb_sb, b.count(1, 1))
                sp.dma_start(comb_dram[b.parity], comb_t[:]).then_inc(comb_out, 16)

            def store_out(b, back=1):
                sp.wait_ge(y_done, b.count(TPB, TPB - TPB * back))
                i = b.of_pair(1, (b.parity - back) // 2)
                sp.dma_start(of_tiles(out_v, i, (b.parity - back) % 2),
                             fin[:].rearrange("p (j d) -> p j d", j=TPB)).then_inc(y_out, 16)

            def load_weights_of_rows(b, n):
                for e, p0, p1 in SPANS[n]:
                    row = comb_dram[b.parity, e * TPB:(e + 1) * TPB, :].rearrange("j t -> (j t)")
                    sp.dma_start(g[n % RING][p0:p1, :], row.partition_broadcast(p1 - p0)).then_inc(cb_in[n % RING], 16)

            def slot(b, c):
                attention(b, c)
                if c == 1:
                    store_comb(b)
                if c == 2:
                    if b.number() == 0:
                        wait_split(sp, PIECES)
                    sp.wait_ge(comb_out, b.count(16, 16))
                    for n in range(SHC, SHC + 3):
                        if n > SHC:
                            wait(sp, glo_done, b.count(NC, n - RING + 1))
                        load_weights_of_rows(b, n)
                n = c + SHC
                if SHC + 2 < n < NC:
                    wait(sp, glo_done, b.count(NC, n - RING + 1))
                    load_weights_of_rows(b, n)
                if c == LAG and b.number() != 0:
                    store_out(b)

            def tail(b):
                store_out(b)
                sp.wait_ge(y_out, 16 * BLOCKS + 1)
                sp.wait_ge(comb_out, 16 * BLOCKS)

            run(sp, prologue, slot, tail, rates=(2, 4, 8, 32, 2 * EXC, 1))

        @block.scalar
        def _(act):
            def split_piece(k):
                cols = piece_cols(k)
                act.wait_ge(piece_in[k % 4], 16 * (k // 4 + 1))
                nc.scalar.activation(w_hi[:, cols], stage[k % 4][:, :cols.stop - cols.start],
                                     ACT.Copy).then_inc(piece_hi, 1)

            def norm_out(norm, t, src):
                act.wait_ge(n_shift[norm], t.done())
                nc.scalar.activation(xn[:], src[:], ACT.Identity, bias=shift[norm][:, 0:1],
                                     scale=rstd[norm][:, 0:1]).then_inc(n_out[norm], 1)

            def nt_hi(ps_done, done, t):
                act.wait_ge(ps_done, t.done())
                nc.scalar.activation(nt[:, 0], pa[:, :D], ACT.Copy).then_inc(done, 1)

            def attention(b, c):
                if (st := slot_tiles(b, c)) is None:
                    return
                s, f, a, r = st
                if s == 0 and f.exists():
                    nt_hi(at_ps, at_hi, f)
                if s == 1 and r.exists():
                    norm_out(0, r, xs[r.ring4])
                if s == 3 and r.exists():
                    wait(act, proj_ps, f.done())
                    nt_hi(n_ps[0], n_hi[0], r)
                if s == 4 and f.exists():
                    norm_out(1, f, x1[f.ring4])
                if s == 5 and a.exists():
                    act.wait_ge(shifted, a.done())
                    nc.scalar.activation(score[:], score[:], ACT.Exp, scale=float(HD) ** -0.5).then_inc(exp_done, 1)
                if s == 5 and f.exists():
                    j = f.ring2
                    act.wait_ge(n_ps[1], f.done())
                    nc.scalar.activation(xt[1 - b.parity][:, 0, :, j * P:(j + 1) * P],
                                         pa[:, :D].rearrange("p (k t) -> p k t", k=KD), ACT.Copy).then_inc(n_hi[1], 1)
                if s == 7 and r.exists():
                    if a.exists():
                        act.wait_ge(prod_done, a.done(per_tile=2 * NG, part=NG))
                    qk_out(r)
                if s == 10 and r.exists():
                    v_out(r)
                if s == 8 and f.exists():
                    j = f.ring2
                    act.wait_ge(gate_ps, f.done())
                    nc.scalar.activation(logit[:, j * E:(j + 1) * E], pa[:, D:D + E], ACT.Copy).then_inc(logit_done, 1)
                if c == PHASE + 8 and f.exists():
                    act.wait_ge(logit_done, f.done())
                    wait(act, comb_done, b.count(1, 1))
                    nc.scalar.activation(sig[:], logit[:], ACT.Exp, scale=-1.0).then_inc(gate_exp, 1)

            def v_out(t):
                act.wait_ge(v_ps, t.done())
                nc.scalar.activation(vt[t.ring2][:].rearrange("p (d h) -> p h d", h=HEADS),
                                     pa[:, :D].rearrange("p (h d) -> p h d", h=HEADS),
                                     ACT.Copy).then_inc(v_sb, 1)

            def qk_out(t):
                act.wait_ge(qk_ps, t.done())
                nc.scalar.activation(qk[:], pb[:], ACT.Copy).then_inc(qk_sb, 1)

            def comb_evacuated(b, c):
                if c == 1:
                    act.wait_ge(comb_ps, b.count(1, 1))
                    wait(act, comb_out, b.count(16, 0))
                    wait(act, glo_done, b.count(NC, SHC + 1 - RING))
                    nc.scalar.activation(comb_t[:], pb[:E * TPB, :P], ACT.Copy).then_inc(comb_sb, 1)

            def prologue(b):
                first = Tile(b, 2)
                norm_out(0, first, xs[0])
                for k in range(PIECES_QKV):
                    split_piece(k)
                nt_hi(n_ps[0], n_hi[0], first)
                qk_out(first)
                v_out(first)
                for k in range(PIECES_QKV, PIECES_ATT):
                    split_piece(k)
                for c, pieces in PROLOGUE:
                    for k in pieces:
                        split_piece(k)
                    attention(b, c)

            def slot(b, c):
                n, r = CHUNK_ROWS[c], c % RING
                act.wait_ge(h_done, b.count(NC, c + 1))
                nc.scalar.activation(act_h[(b.parity + c) % 2][:n], h[r][:n, :BT], ACT.Silu).then_inc(silu_done, 1)
                comb_evacuated(b, c)
                attention(b, c)
                ghi(b, c, 1)

            def ghi(b, c, lag):
                exists, n, r = behind(b, c, lag)
                if exists:
                    act.wait_ge(g_done, b.count(NC, c + 1 - lag))
                    nc.scalar.activation(g_hi[r][:n], g[r][:n], ACT.Copy).then_inc(ghi_done, 1)

            def tail(b):
                ghi(b, 0, 1)

            run(act, prologue, slot, tail)

        @block.gpsimd
        def _(pool):
            def split_piece(k):
                cols = piece_cols(k)
                n = cols.stop - cols.start
                pool.wait_ge(piece_hi, k + 1)
                nc.gpsimd.tensor_tensor(w_lo[:, cols], stage[k % 4][:, :n], w_hi[:, cols].bitcast(F32),
                                        ALU.subtract).then_inc(piece_lo, 1)

            def norm_factors(norm, t):
                pool.wait_ge(n_var[norm], t.done())
                nc.gpsimd.tensor_tensor(rstd[norm][:], var[norm][:], neg_half[:], ALU.pow).then_inc(n_rstd[norm], 1)
                nc.gpsimd.tensor_tensor(minus[norm][:], mv[norm][:, 0:1], neg_one[:], ALU.mult).then_inc(n_rstd[norm], 1)
                pool.wait_ge(n_rstd[norm], t.done(per_tile=2))
                nc.gpsimd.tensor_tensor(shift[norm][:], minus[norm][:], rstd[norm][:], ALU.mult).then_inc(n_shift[norm], 1)

            def x_plus_bias(t):
                pool.wait_ge(n_out[0], t.done())
                nc.gpsimd.tensor_tensor(xs[t.ring4][:], xs[t.ring4][:], bias[:], ALU.add).then_inc(xb_done, 1)

            def attention(b, c):
                if (st := slot_tiles(b, c)) is None:
                    return
                s, f, a, r = st
                if s == 0 and r.exists():
                    norm_factors(0, r)
                if s == 2 and r.exists():
                    x_plus_bias(r)
                if s == 4 and a.exists():
                    s3 = score[:].rearrange("p (h g) -> p h g", h=HEADS)
                    pool.wait_ge(top_done, a.done())
                    nc.gpsimd.tensor_tensor(s3, s3, top[:, :, None].broadcast_to([P, HEADS, HEADS]),
                                            ALU.subtract).then_inc(shifted, 1)
                if s == 10 and a.exists():
                    a3 = att[:].rearrange("p (h d) -> p h d", h=HEADS)
                    pool.wait_ge(red_done, a.done(per_tile=2 * NG))
                    pool.wait_ge(rden_done, a.done())
                    nc.gpsimd.tensor_tensor(a3, a3, rden[:, :, None].broadcast_to([P, HEADS, HD]),
                                            ALU.mult).then_inc(att_done, 1)

            def prologue(b):
                nc.gpsimd.memset(neg_half[:], -0.5).then_inc(consts, 1)
                nc.gpsimd.memset(neg_one[:], -1.0).then_inc(consts, 1)
                nc.gpsimd.memset(ident[:], 0.0).then_inc(consts, 1)
                pool.wait_ge(consts, 3)
                pool.affine_select(out=ident[:], in_=ident[:], compare_op=ALU.not_equal, fill=1.0, base=0,
                                   pattern=[[-1, P]], channel_multiplier=1).then_inc(consts, 1)
                first = Tile(b, 2)
                norm_factors(0, first)
                pool.wait_ge(bias_in, 16)
                x_plus_bias(first)
                for k in range(PIECES_QKV, PIECES_ATT):
                    split_piece(k)
                for c, pieces in PROLOGUE:
                    second_norm_factors(b, c)
                    attention(b, c)
                    for k in pieces:
                        split_piece(k)

            def second_norm_factors(b, c):
                if (st := slot_tiles(b, c)) is not None and st[0] == 4 and st[1].exists():
                    norm_factors(1, st[1])

            def slot(b, c):
                second_norm_factors(b, c)
                if c >= SHC:
                    r = c % RING
                    pool.wait_ge(silu_done, b.count(NC, c + 1))
                    pool.wait_ge(cb_in[r], b.count(16 * CB_ALL[r], 16 * CB_UPTO[c]))
                    nc.gpsimd.tensor_tensor(g[r], act_h[(b.parity + c) % 2][:], g[r], ALU.mult).then_inc(weighted, 1)
                attention(b, c)
                glo(b, c, 1)

            def glo(b, c, lag):
                exists, n, r = behind(b, c, lag)
                if exists:
                    pool.wait_ge(ghi_done, b.count(NC, c + 1 - lag))
                    nc.gpsimd.tensor_tensor(g_lo[r][:n], g[r][:n], g_hi[r][:n].bitcast(F32),
                                            ALU.subtract).then_inc(glo_done, 1)

            def tail(b):
                glo(b, 0, 1)

            run(pool, prologue, slot, tail)

        @block.vector
        def _(dve):
            vec = nc.vector

            def carry_wait():
                vec.memset(hold[:], 0.0)

            def norm_stats(norm, t, src):
                vec.bn_stats(stats[norm][:], src[:]).then_inc(n_stats[norm], 1)

            def norm_var(norm, t):
                dve.wait_ge(n_stats[norm], t.done())
                wait(dve, n_shift[norm], t.done(back=1))
                carry_wait()
                vec.bn_aggr(mv[norm][:], stats[norm][:]).then_inc(n_mv[norm], 1)
                dve.wait_ge(n_mv[norm], t.done())
                vec.tensor_scalar(var[norm][:], mv[norm][:, 1:2], EPS, None, ALU.add).then_inc(n_var[norm], 1)

            def product(t, n):
                i = n % NG
                heads = slice(i * GROUP * HD, (i + 1) * GROUP * HD)
                if n == 0:
                    dve.wait_ge(qk_sb, t.done())
                if n == NG:
                    dve.wait_ge(exp_done, t.done())
                    dve.wait_ge(v_sb, t.done())
                wait(dve, red_done, t.done(per_tile=2 * NG, part=2 * NG + 1 - n))
                left = (qk[:, heads] if n < NG else score[:, heads]).rearrange("p (h d) -> p h d", h=GROUP)
                right = (qk[:, D:] if n < NG else vt[t.ring2][:]).rearrange("p (h d) -> p h d", h=HEADS)
                shape = [P, GROUP, HEADS, HD]
                vec.tensor_tensor(prod[n % 2][:].rearrange("p (g h d) -> p g h d", g=GROUP, h=HEADS),
                                  left[:, :, None, :].broadcast_to(shape), right[:, None, :, :].broadcast_to(shape),
                                  ALU.mult).then_inc(prod_done, 1)

            def reduced(t, n):
                i = n % NG
                to = (score if n < NG else att)[:, i * GROUP * HD:(i + 1) * GROUP * HD]
                dve.wait_ge(prod_done, t.done(per_tile=2 * NG, part=2 * NG - 1 - n))
                if n == NG:
                    wait(dve, at_ps, t.done(back=1))
                vec.tensor_reduce(to, prod[n % 2][:].rearrange("p (x d) -> p x d", d=HD), AX.X, ALU.add).then_inc(red_done, 1)

            def maximum(t):
                dve.wait_ge(red_done, t.done(per_tile=2 * NG, part=NG))
                vec.tensor_reduce(top[:], score[:].rearrange("p (h g) -> p h g", h=HEADS), AX.X, ALU.max).then_inc(top_done, 1)

            def denominator(t):
                dve.wait_ge(exp_done, t.done())
                vec.tensor_reduce(den[:], score[:].rearrange("p (h g) -> p h g", h=HEADS), AX.X,
                                  ALU.add).then_inc(den_done, 1)

            def inverse_denominator(t):
                dve.wait_ge(den_done, t.done())
                vec.reciprocal(rden[:], den[:]).then_inc(rden_done, 1)

            def residual(t):
                dve.wait_ge(proj_ps, t.done())
                dve.wait_ge(xb_done, t.done())
                vec.tensor_tensor(x1[t.ring4], pb[:, :D], xs[t.ring4][:], ALU.add).then_inc(x1_done, 1)

            def nt_lo(hi_done, done, t):
                dve.wait_ge(hi_done, t.done())
                vec.tensor_tensor(nt[:, 1], pa[:, :D], nt[:, 0].bitcast(F32), ALU.subtract).then_inc(done, 1)

            def attention_before(b, c):
                if (st := slot_tiles(b, c)) is None:
                    return
                s, f, a, r = st
                n = Tile(b, r.offset + 1)
                if s == 5 and n.exists():
                    dve.wait_ge(x_in[n.ring4], n.dma())
                    norm_stats(0, n, xs[n.ring4])
                if s == 1 and f.exists():
                    nt_lo(at_hi, at_lo, f)
                if c == LAG - 1 and b.number() not in (-1, 0):
                    finish(b)
                if s == 3 and f.exists():
                    if c == 3:
                        wait(dve, y_done, b.count(TPB, 0))
                    residual(f)
                    dve.wait_ge(x1_done, f.done())
                    norm_stats(1, f, x1[f.ring4])
                if s == 11 and r.exists():
                    product(r, 0)
                if a.exists():
                    if s == 0:
                        product(a, 1)
                    if s == 1:
                        product(a, 2)
                    if s == 2:
                        reduced(a, 1)
                    if s == 6:
                        denominator(a)
                        product(a, 4)
                    if s == 7:
                        reduced(a, 4)
                    if s == 8:
                        reduced(a, 5)
                    if s == 9:
                        reduced(a, 6)
                    if s == 10:
                        reduced(a, 7)

            def attention_behind(b, c):
                if (st := slot_tiles(b, c)) is None:
                    return
                s, f, a, r = st
                n = Tile(b, r.offset + 1)
                if s == 5 and n.exists():
                    norm_var(0, n)
                if s == 6 and f.exists():
                    j = f.ring2
                    part = (slice(None), slice(None), slice(j * P, (j + 1) * P))
                    dve.wait_ge(n_hi[1], f.done())
                    vec.tensor_tensor(xt[1 - b.parity][:, 1][part], pa[:, :D].rearrange("p (k t) -> p k t", k=KD),
                                      xt[1 - b.parity][:, 0][part].bitcast(F32), ALU.subtract).then_inc(n_lo[1], 1)
                if s == 3 and r.exists():
                    nt_lo(n_hi[0], n_lo[0], r)
                if s == 3 and f.exists():
                    norm_var(1, f)
                if a.exists():
                    if s == 0:
                        reduced(a, 0)
                    if s == 2:
                        product(a, 3)
                    if s == 3:
                        reduced(a, 2)
                    if s == 4:
                        reduced(a, 3)
                        maximum(a)
                    if s == 6:
                        product(a, 5)
                        inverse_denominator(a)
                    if s == 7:
                        product(a, 6)
                    if s == 8:
                        product(a, 7)

            ROUTE_FROM = PHASE + 9
            ROUTE_PLACES = 5
            ROUTE = 14

            def routing(b, c, place):
                step = (c - ROUTE_FROM) * ROUTE_PLACES + place
                if not 0 <= step <= ROUTE or not Tile(b, TPB).exists():
                    return
                by_group = sig[:].rearrange("p (j g e) -> p j g e", j=TPB, g=4)
                w3 = wsel[:].rearrange("p (j e) -> p j e", j=TPB)
                if step == 0:
                    dve.wait_ge(gate_exp, b.count(1, 2))
                else:
                    dve.wait_ge(route, b.count(ROUTE, ROUTE + step))
                if step in (3, 5, 8, 10):
                    carry_wait()
                if step == 0:
                    last = vec.tensor_scalar(sig[:], sig[:], 1.0, None, ALU.add)
                if step == 1:
                    last = vec.reciprocal(sig[:], sig[:])
                if step == 2:
                    last = vec.tensor_reduce(gpick[:, :, 0:4], by_group, AX.X, ALU.max)
                if step == 3:
                    for j in range(TPB):
                        last = vec.max(best[:, j], gpick[:, j])
                if step == 4:
                    last = vec.memset(best[:, :, 2:], -1.0)
                if step == 5:
                    for j in range(TPB):
                        last = vec.match_replace(left[:, j, 0:10], best[:, j], gpick[:, j], -9.0)
                if step == 6:
                    last = vec.tensor_scalar(gsel[:].rearrange("p (j g) -> p j g", j=TPB), left[:, :, 0:4], -2.0, None, ALU.is_lt)
                if step == 7:
                    last = vec.tensor_tensor(epick[:, :, 0:E].rearrange("p j (g e) -> p j g e", g=4), by_group,
                                             gsel[:].rearrange("p (j g) -> p j g", j=TPB)[:, :, :, None].broadcast_to([P, TPB, 4, 4]),
                                             ALU.mult)
                if step == 8:
                    for j in range(TPB):
                        last = vec.max(best[:, j], epick[:, j])
                if step == 9:
                    last = vec.memset(best[:, :, 4:], -1.0)
                if step == 10:
                    for j in range(TPB):
                        last = vec.match_replace(left[:, j], best[:, j], epick[:, j], -9.0)
                if step == 11:
                    last = vec.scalar_tensor_tensor(w3, left[:, :, 0:E], -2.0, sig[:].rearrange("p (j e) -> p j e", j=TPB),
                                                    ALU.is_lt, ALU.mult)
                if step == 12:
                    last = vec.tensor_reduce(wden[:], w3, AX.X, ALU.add)
                if step == 13:
                    last = vec.reciprocal(wden[:], wden[:])
                if step < ROUTE:
                    last.then_inc(route, 1)
                else:
                    wait(dve, comb_ps, b.count(1, 1))
                    vec.tensor_tensor(comb[:].rearrange("p (e j) -> p j e", j=TPB), w3,
                                      wden[:, :, None].broadcast_to([P, TPB, E]), ALU.mult).then_inc(comb_done, 1)

            def split_piece(k):
                cols = piece_cols(k)
                dve.wait_ge(piece_hi, k + 1)
                vec.tensor_tensor(w_lo[:, cols], stage[k % 4][:, :cols.stop - cols.start],
                                  w_hi[:, cols].bitcast(F32), ALU.subtract).then_inc(piece_lo_v, 1)

            def prologue(b):
                vec.memset(gpick[:, :, 4:], -1.0)
                vec.memset(epick[:, :, E:], -1.0).then_inc(y_out, 1)
                dve.wait_ge(y_out, 1)
                first = Tile(b, 2)
                dve.wait_ge(x_in[0], 16)
                norm_stats(0, first, xs[0])
                norm_var(0, first)
                dve.wait_ge(x_in[1], 16)
                norm_stats(0, Tile(b, 3), xs[1])
                for k in range(PIECES_QKV):
                    split_piece(k)
                nt_lo(n_hi[0], n_lo[0], first)
                product(first, 0)
                norm_var(0, Tile(b, 3))
                for c, _ in PROLOGUE:
                    routing(b, c, 0)
                    attention_before(b, c)
                    routing(b, c, 1)
                    routing(b, c, 2)
                    attention_behind(b, c)
                    routing(b, c, 3)
                    routing(b, c, 4)

            def finish(b):
                dve.wait_ge(down_done, b.count(NC, 0))
                dve.wait_ge(y_out, b.count(16, 1 - 16))
                for j in range(TPB):
                    at = slice(j * D, (j + 1) * D)
                    vec.tensor_tensor(fin[:, at], y[:, at], x1[(TPB * (1 - b.parity) + j) % TPP], ALU.add).then_inc(y_done, 1)

            def gate(b, c, lag):
                exists, n, r = behind(b, c, lag)
                if exists:
                    dve.wait_ge(h_done, b.count(NC, c + 1 - lag))
                    left = g[r]
                    if 0 <= c - lag < SHC:
                        dve.wait_ge(silu_done, b.count(NC, c + 1 - lag))
                        wait(dve, glo_done, b.count(NC, c + 1 - lag - RING))
                        left = act_h[(b.parity + c - lag) % 2]
                    else:
                        dve.wait_ge(weighted, routed_upto(b, c - lag))
                    vec.tensor_tensor(g[r][:n], left[:n], h[r][:n, BT:], ALU.mult).then_inc(g_done, 1)

            def slot(b, c):
                if c == 1 and b.number() == 0:
                    wait_split(dve, PIECES)
                routing(b, c, 0)
                attention_before(b, c)
                routing(b, c, 1)
                gate(b, c, 1)
                routing(b, c, 2)
                attention_behind(b, c)
                routing(b, c, 3)
                routing(b, c, 4)

            def tail(b):
                gate(b, 0, 1)
                finish(b)

            run(dve, prologue, slot, tail)

        @block.tensor
        def _(pe):
            mm = nc.tensor.matmul

            def product(to, left, right, **kw):
                for n, (lp, rp) in enumerate(((0, 0), (0, 1), (1, 0))):
                    for k in range(KD):
                        last = mm(to, left(lp, k), right(rp, k), start=(n == 0 and k == 0), stop=(n == 2 and k == KD - 1), **kw)
                return last

            def weight(at, width, first, count):
                return lambda part, k: (w_hi, w_lo)[part][:, at + k * width + first:at + k * width + first + count]

            def of_nt(part, k):
                return nt[:, part, k * P:(k + 1) * P]

            def transposes(src):
                for k in range(KD):
                    last = nc.tensor.transpose(pa[:, k * P:(k + 1) * P], src[:, k * P:(k + 1) * P], ident[:])
                return last

            def n1_transposed(t):
                pe.wait_ge(n_out[0], t.done())
                transposes(xn).then_inc(n_ps[0], 1)

            def qk_product(t):
                pe.wait_ge(n_lo[0], t.done())
                product(pb[:], of_nt, weight(AT_QKV, 3 * D, 0, 2 * D)).then_inc(qk_ps, 1)

            def v_product(t):
                product(pa[:, :D], of_nt, weight(AT_QKV, 3 * D, 2 * D, D)).then_inc(v_ps, 1)

            def attention(b, c):
                if (st := slot_tiles(b, c)) is None:
                    return
                s, f, a, r = st
                if s == 3 and r.exists():
                    if not f.exists():
                        wait(pe, v_sb, r.done(back=1))
                    n1_transposed(r)

            def attention_behind(b, c):
                if (st := slot_tiles(b, c)) is None:
                    return
                s, f, a, r = st
                before = Tile(b, f.offset - 1)
                if s == 0 and f.exists():
                    pe.wait_ge(att_done, f.done())
                    if a.exists():
                        pe.wait_ge(v_sb, a.done())
                    else:
                        pe.wait_ge(logit_done, before.done())
                    transposes(att).then_inc(at_ps, 1)
                if s == 2 and f.exists():
                    if c == 2 and b.number() != -1:
                        pe.wait_ge(comb_sb, b.count(1, 1))
                    elif a.exists():
                        pe.wait_ge(qk_sb, a.done())
                    else:
                        pe.wait_ge(x1_done, before.done())
                    pe.wait_ge(at_lo, f.done())
                    product(pb[:, :D], of_nt, weight(AT_WO, D, 0, D)).then_inc(proj_ps, 1)
                if s == 6 and f.exists():
                    if r.exists():
                        pe.wait_ge(n_lo[0], r.done())
                    pe.wait_ge(n_out[1], f.done())
                    transposes(xn).then_inc(n_ps[1], 1)
                if s == 6 and r.exists():
                    if f.exists():
                        pe.wait_ge(x1_done, f.done())
                    else:
                        wait(pe, qk_sb, r.done(back=1))
                    qk_product(r)
                if s == 8 and f.exists():
                    j, par = f.ring2, 1 - b.parity
                    pe.wait_ge(n_lo[1], f.done())
                    product(pa[:, D:D + E], lambda part, k: xt[par][:, part, k, j * P:(j + 1) * P],
                            weight(AT_GATE, E, 0, E)).then_inc(gate_ps, 1)
                if s == 9 and r.exists():
                    if f.exists():
                        pe.wait_ge(logit_done, f.done())
                    v_product(r)

            def comb_transposed(b, c):
                if c == 1:
                    pe.wait_ge(comb_done, b.count(1, 1))
                    if Tile(b, 3).exists():
                        pe.wait_ge(qk_sb, Tile(b, 3).done())
                    else:
                        pe.wait_ge(x1_done, Tile(b, 1).done())
                    mm(pb[:E * TPB, :P], comb[:], ident[:], start=True, stop=True).then_inc(comb_ps, 1)

            def prologue(b):
                first = Tile(b, 2)
                pe.wait_ge(consts, 4)
                n1_transposed(first)
                wait_split(pe, PIECES_QKV)
                qk_product(first)
                v_product(first)
                wait_split(pe, PIECES_ATT)
                for c, _ in PROLOGUE:
                    attention(b, c)
                    attention_behind(b, c)

            def rows(b, c):
                n, at, r, par = CHUNK_ROWS[c], AT_CHUNK[c], c % RING, b.parity
                if b.number() == 0 and c < LAG:
                    wait_split(pe, pieces_until(AT_CHUNK[c + 1]))
                if b.number() == 0 and c == LAG:
                    wait_split(pe, PIECES)
                if c == 0:
                    pe.wait_ge(n_lo[1], b.count(TPB, TPB))
                wait(pe, g_done, b.count(NC, c + 1 - RING))
                for to, w_at in ((h[r][:n, :BT], at), (h[r][:n, BT:], at + KD * n)):
                    last = product(to, weight(w_at, n, 0, n), lambda part, k: xt[par][:, part, k, :])
                last.then_inc(h_done, 1)

            def down(b, c, lag):
                exists, n, r = behind(b, c, lag)
                if not exists:
                    return
                chunk = (c - lag) % NC
                pe.wait_ge(glo_done, b.count(NC, c + 1 - lag))
                if chunk == 0:
                    wait(pe, y_done, b.count(TPB, 0))
                w = slice(AT_CHUNK[chunk + 1] - D, AT_CHUNK[chunk + 1])
                for j in range(TPB):
                    tok = slice(j * P, (j + 1) * P)
                    for m, (gp, wp) in enumerate(((g_hi[r], w_hi), (g_hi[r], w_lo), (g_lo[r], w_hi))):
                        last = mm(y[:, j * D:(j + 1) * D], gp[:n, tok], wp[:n, w],
                                  start=(chunk == 0 and j == 0 and m == 0),
                                  stop=(chunk == NC - 1 and j == TPB - 1 and m == 2), skip_group_check=True)
                last.then_inc(down_done, 1)

            def slot(b, c):
                rows(b, c)
                comb_transposed(b, c)
                attention(b, c)
                down(b, c, LAG)
                attention_behind(b, c)

            def tail(b):
                for c in range(LAG):
                    down(b, c, LAG)

            run(pe, prologue, slot, tail)


def kernel(L0_attn_x, L0_attn_W_qkv, L0_attn_W_out, L0_attn_b_out, L0_ffn_gate_w, L0_ffn_W1, L0_ffn_W2,
           L0_ffn_W3, L0_ffn_Ws1, L0_ffn_Ws2, L0_ffn_Ws3):
    import numpy as np
    import concourse.bacc as bacc
    from concourse.bass_utils import run_bass_kernel_spmd

    def by_contraction(w):
        w = np.asarray(w)
        return w.reshape(KD, P, w.shape[1]).transpose(1, 0, 2).reshape(P, -1)

    w1 = np.concatenate([np.asarray(L0_ffn_Ws1), np.asarray(L0_ffn_W1).reshape(E * I, D)])
    w3 = np.concatenate([np.asarray(L0_ffn_Ws3), np.asarray(L0_ffn_W3).reshape(E * I, D)])
    w2 = np.concatenate([np.asarray(L0_ffn_Ws2).T, np.asarray(L0_ffn_W2).transpose(0, 2, 1).reshape(E * I, D)])
    parts = [by_contraction(L0_attn_W_qkv), by_contraction(L0_attn_W_out), by_contraction(np.asarray(L0_ffn_gate_w).T)]
    first = 0
    for rows in CHUNK_ROWS:
        chunk = slice(first, first + rows)
        pad = np.zeros((P - rows, D), w2.dtype)
        parts += [by_contraction(w1[chunk].T), by_contraction(w3[chunk].T), np.concatenate([w2[chunk], pad])]
        first += rows
    packed = np.concatenate(parts, axis=1)
    assert packed.shape == (P, WCOLS)
    arrays = {
        "x": np.ascontiguousarray(np.asarray(L0_attn_x).reshape(T, D)),
        "weights": np.ascontiguousarray(packed),
        "b_out": np.ascontiguousarray(np.asarray(L0_attn_b_out)),
    }
    nc = bacc.Bacc("TRN2", target_bir_lowering=False, num_devices=1, dynamic_dma_scratch_size=512)
    ins = [nc.dram_tensor(n, a.shape, mybir.dt.from_np(a.dtype), kind="ExternalInput").ap() for n, a in arrays.items()]
    comb = nc.dram_tensor("comb_by_expert", (2, E * TPB, P), F32, kind="Internal").ap()
    out = nc.dram_tensor("out", (T, D), F32, kind="ExternalOutput").ap()
    build(nc, *ins, comb, out)
    r = run_bass_kernel_spmd(nc, [arrays], core_ids=[0])
    return r.results[0]["out"].reshape(np.asarray(L0_attn_x).shape)
```
